# Optimizing a Trainium2 kernel written in Bass

```python
import numpy as np
import jax
import jax.numpy as jnp

def _softmax(x, axis=-1):
    return jax.nn.softmax(x, axis=axis)

def _gelu(x):
    return jax.nn.gelu(x, approximate=True)

def _silu(x):
    return jax.nn.silu(x)

def _sigmoid(x):
    return jax.nn.sigmoid(x)

def _layernorm(x, axis=-1, eps=1e-05):
    m = jnp.mean(x, axis=axis, keepdims=True)
    v = jnp.var(x, axis=axis, keepdims=True)
    return (x - m) / jnp.sqrt(v + eps)

def _scatter_add(tgt, idx, src, axis=0):
    return tgt.at[idx].add(src)

def _segment_sum(src, seg, n):
    return jax.ops.segment_sum(src, seg, n)
kernel_name = 'mk_adj_resnorm_d4_adj_r2_df7eb8'

def setup_inputs(seed: int=0):
    np.random.seed(seed)
    _w = jnp.asarray

    def _rec_inputs():
        import jax
        import jax.numpy as jnp
        _gk = jax.random.key(seed)
        x = -0.0002928 + 1 * jax.random.normal(jax.random.fold_in(_gk, 1), (64, 128, 128), jnp.float32)
        _a = jax.random.bernoulli(jax.random.fold_in(_gk, 2), 0.03125, (64, 128, 128))
        adj = _a.astype(jnp.int32)
        return (x, adj)
    x, adj = _rec_inputs()

    def _L0_gnn_setup():
        import jax, jax.numpy as jnp
        import numpy as np
        NEG_INF = -9000000000000000.0
        ALPHA = 0.2
        key = jax.random.key(seed)
        k1, k2, k3, k4 = jax.random.split(key, 4)
        B, N, Fin, Fout = (8, 1024, 128, 128)
        h = jax.random.normal(k1, (B, N, Fin), dtype=jnp.float32)
        adj = jax.random.randint(k2, (B, N, N), 0, 2, dtype=jnp.int32)
        W = jax.random.normal(k3, (Fout, Fin), dtype=jnp.float32) / np.sqrt(Fin)
        a = jax.random.normal(k4, (2 * Fout,), dtype=jnp.float32) / np.sqrt(2 * Fout)
        return {'h': h, 'adj': adj, 'W': W, 'a': a}
    _L0_gnn_all = _L0_gnn_setup()
    _L0_gnn_in = {k: v for k, v in _L0_gnn_all.items() if k in ('W', 'a')}
    del _L0_gnn_all

    def _L1_gnn_setup():
        import jax, jax.numpy as jnp
        import numpy as np
        OUT = 128
        NUM_LAYERS = 3

        def _gru_cell(inp, h, w_ih, w_hh, b_ih, b_hh):
            gi = inp @ w_ih.T + b_ih
            gh = h @ w_hh.T + b_hh
            i_r, i_z, i_n = jnp.split(gi, 3, axis=-1)
            h_r, h_z, h_n = jnp.split(gh, 3, axis=-1)
            r = jax.nn.sigmoid(i_r + h_r)
            z = jax.nn.sigmoid(i_z + h_z)
            n = jnp.tanh(i_n + r * h_n)
            return (1.0 - z) * n + z * h
        key = jax.random.key(seed)
        ks = jax.random.split(key, 8)
        B, N, D = (32, 256, 128)
        x = jax.random.normal(ks[0], (B, N, D), dtype=jnp.float32)
        adj = jax.random.randint(ks[1], (B, N, N), 0, 2, dtype=jnp.int32)
        s = 1.0 / np.sqrt(OUT)
        weight = jax.random.uniform(ks[2], (NUM_LAYERS, OUT, OUT), jnp.float32, -s, s)
        w_ih = jax.random.uniform(ks[3], (3 * OUT, OUT), jnp.float32, -s, s)
        w_hh = jax.random.uniform(ks[4], (3 * OUT, OUT), jnp.float32, -s, s)
        b_ih = jax.random.uniform(ks[5], (3 * OUT,), jnp.float32, -s, s)
        b_hh = jax.random.uniform(ks[6], (3 * OUT,), jnp.float32, -s, s)
        return {'x': x, 'adj': adj, 'weight': weight, 'w_ih': w_ih, 'w_hh': w_hh, 'b_ih': b_ih, 'b_hh': b_hh}
    _L1_gnn_all = _L1_gnn_setup()
    _L1_gnn_in = {k: v for k, v in _L1_gnn_all.items() if k in ('weight', 'w_ih', 'w_hh', 'b_ih', 'b_hh')}
    del _L1_gnn_all

    def _L2_gnn_setup():
        import jax, jax.numpy as jnp
        import numpy as np
        NEG_INF = -1000000000.0
        LEAKY_ALPHA = 0.2
        key = jax.random.key(seed)
        k1, k2, k3, k4 = jax.random.split(key, 4)
        B, N, Din, Dout = (16, 1024, 128, 128)
        h = jax.random.normal(k1, (B, N, Din), dtype=jnp.float32)
        adj = jax.random.randint(k2, (B, N, N), 0, 2, dtype=jnp.int32)
        W = jax.random.normal(k3, (Din, Dout), dtype=jnp.float32) * (1.0 / np.sqrt(Din))
        a = jax.random.normal(k4, (2 * Dout,), dtype=jnp.float32) * (1.0 / np.sqrt(2 * Dout))
        return {'h': h, 'adj': adj, 'W': W, 'a': a}
    _L2_gnn_all = _L2_gnn_setup()
    _L2_gnn_in = {k: v for k, v in _L2_gnn_all.items() if k in ('W', 'a')}
    del _L2_gnn_all

    def _L3_gnn_setup():
        import jax, jax.numpy as jnp
        import numpy as np
        B, S, D = (64, 256, 128)

        def _leaky(x):
            return jnp.where(x >= 0, x, 0.2 * x)
        key = jax.random.key(seed)
        k = jax.random.split(key, 6)
        stdv = 1.0 / np.sqrt(D)
        return {'hidden': jax.random.normal(k[0], (B, S, D), dtype=jnp.float32), 'adj': jax.random.randint(k[1], (B, S, S), 0, 5, dtype=jnp.int32), 'a0': jax.random.uniform(k[2], (D, 1), jnp.float32, -stdv, stdv), 'a1': jax.random.uniform(k[3], (D, 1), jnp.float32, -stdv, stdv), 'a2': jax.random.uniform(k[4], (D, 1), jnp.float32, -stdv, stdv), 'a3': jax.random.uniform(k[5], (D, 1), jnp.float32, -stdv, stdv), 'bias': jnp.zeros((D,), dtype=jnp.float32)}
    _L3_gnn_all = _L3_gnn_setup()
    _L3_gnn_in = {k: v for k, v in _L3_gnn_all.items() if k in ('a0', 'a1', 'a2', 'a3', 'bias')}
    del _L3_gnn_all
    return {'x': x, 'adj': adj, 'L0_gnn_W': _L0_gnn_in['W'], 'L0_gnn_a': _L0_gnn_in['a'], 'L1_gnn_weight': _L1_gnn_in['weight'], 'L1_gnn_w_ih': _L1_gnn_in['w_ih'], 'L1_gnn_w_hh': _L1_gnn_in['w_hh'], 'L1_gnn_b_ih': _L1_gnn_in['b_ih'], 'L1_gnn_b_hh': _L1_gnn_in['b_hh'], 'L2_gnn_W': _L2_gnn_in['W'], 'L2_gnn_a': _L2_gnn_in['a'], 'L3_gnn_a0': _L3_gnn_in['a0'], 'L3_gnn_a1': _L3_gnn_in['a1'], 'L3_gnn_a2': _L3_gnn_in['a2'], 'L3_gnn_a3': _L3_gnn_in['a3'], 'L3_gnn_bias': _L3_gnn_in['bias']}

def reference(x, adj, L0_gnn_W, L0_gnn_a, L1_gnn_weight, L1_gnn_w_ih, L1_gnn_w_hh, L1_gnn_b_ih, L1_gnn_b_hh, L2_gnn_W, L2_gnn_a, L3_gnn_a0, L3_gnn_a1, L3_gnn_a2, L3_gnn_a3, L3_gnn_bias):
    import jax
    import jax.numpy as jnp

    def _L0_gnn_ref(h, adj, W, a):
        import jax, jax.numpy as jnp
        import numpy as np
        NEG_INF = -9000000000000000.0
        ALPHA = 0.2
        Wh = jnp.einsum('bnf,of->bno', h, W)
        Fout = Wh.shape[-1]
        a1, a2 = (a[:Fout], a[Fout:])
        f_i = Wh @ a1
        f_j = Wh @ a2
        e = f_i[:, :, None] + f_j[:, None, :]
        e = jnp.where(e > 0, e, ALPHA * e)
        e = jnp.where(adj == 0, NEG_INF, e)
        attention = jax.nn.softmax(e, axis=2)
        h_prime = jnp.einsum('bij,bjo->bio', attention, Wh)
        return h_prime

    def _L1_gnn_ref(x, adj, weight, w_ih, w_hh, b_ih, b_hh):
        import jax, jax.numpy as jnp
        import numpy as np
        OUT = 128
        NUM_LAYERS = 3

        def _gru_cell(inp, h, w_ih, w_hh, b_ih, b_hh):
            gi = inp @ w_ih.T + b_ih
            gh = h @ w_hh.T + b_hh
            i_r, i_z, i_n = jnp.split(gi, 3, axis=-1)
            h_r, h_z, h_n = jnp.split(gh, 3, axis=-1)
            r = jax.nn.sigmoid(i_r + h_r)
            z = jax.nn.sigmoid(i_z + h_z)
            n = jnp.tanh(i_n + r * h_n)
            return (1.0 - z) * n + z * h
        A = (adj != 0).astype(x.dtype)
        h = x
        L = weight.shape[0]
        for i in range(L):
            m = jnp.einsum('bnd,de->bne', h, weight[i])
            aggr = jnp.einsum('bst,bsd->btd', A, m)
            h = _gru_cell(aggr, h, w_ih, w_hh, b_ih, b_hh)
        return h

    def _L2_gnn_ref(h, adj, W, a):
        import jax, jax.numpy as jnp
        import numpy as np
        NEG_INF = -1000000000.0
        LEAKY_ALPHA = 0.2
        Wh = jnp.einsum('bnd,de->bne', h, W)
        Dout = Wh.shape[-1]
        a1, a2 = (a[:Dout], a[Dout:])
        f_i = Wh @ a1
        f_j = Wh @ a2
        e = f_i[:, :, None] + f_j[:, None, :]
        e = jax.nn.leaky_relu(e, negative_slope=LEAKY_ALPHA)
        e = jnp.where(adj > 0, e, NEG_INF)
        alpha = jax.nn.softmax(e, axis=-1)
        out = jnp.einsum('bij,bjd->bid', alpha, Wh)
        return jax.nn.elu(out)

    def _L3_gnn_ref(hidden, adj, a0, a1, a2, a3, bias):
        import jax, jax.numpy as jnp
        import numpy as np
        B, S, D = (64, 256, 128)

        def _leaky(x):
            return jnp.where(x >= 0, x, 0.2 * x)
        h = hidden

        def e_of(a):
            return _leaky(jnp.einsum('bid,bjd->bij', h * a[:, 0], h))
        e0, e1, e2, e3 = (e_of(a0), e_of(a1), e_of(a2), e_of(a3))
        neg_inf = jnp.float32(-jnp.finfo(e0.dtype).max)
        alpha = jnp.where(adj == 1, e0, neg_inf)
        alpha = jnp.where(adj == 2, e1, alpha)
        alpha = jnp.where(adj == 3, e2, alpha)
        alpha = jnp.where(adj == 4, e3, alpha)
        alpha = jax.nn.sigmoid(alpha)
        return jnp.einsum('bij,bjd->bid', alpha, h) + bias
    x = _layernorm(x + _L0_gnn_ref(x, adj, L0_gnn_W, L0_gnn_a), axis=-1)
    x = _layernorm(x + _L1_gnn_ref(x, adj, L1_gnn_weight, L1_gnn_w_ih, L1_gnn_w_hh, L1_gnn_b_ih, L1_gnn_b_hh), axis=-1)
    x = _layernorm(x + _L2_gnn_ref(x, adj, L2_gnn_W, L2_gnn_a), axis=-1)
    x = _layernorm(x + _L3_gnn_ref(x, adj, L3_gnn_a0, L3_gnn_a1, L3_gnn_a2, L3_gnn_a3, L3_gnn_bias), axis=-1)
    return x

_drawn_inputs = setup_inputs


def setup_inputs(seed=0):
    import zlib

    import numpy as np

    out = dict(_drawn_inputs(seed))
    spreads = {'L3_gnn_bias': (0.0, 0.1)}
    factors = {}
    for name, (base, spread) in spreads.items():
        noise = np.random.default_rng([zlib.crc32(name.encode()), seed]).standard_normal(out[name].shape)
        drawn = base * np.exp(spread * noise) if base else spread * noise
        out[name] = jnp.asarray(drawn.astype(out[name].dtype))
    for name, factor in factors.items():
        out[name] = (out[name] * factor).astype(out[name].dtype)
    return out
```

```python
from contextlib import ExitStack

import concourse.bass as bass
from concourse import mybir

F32 = mybir.dt.float32
F16 = mybir.dt.float16
BF16 = mybir.dt.bfloat16
U8 = mybir.dt.uint8
I32 = mybir.dt.int32
ALU = mybir.AluOpType
ACT = mybir.ActivationFunctionType
AX = mybir.AxisListType

P = 128
B = 64
GB = 4
NG = B // GB
PAIRS = NG // 2
GW = GB * P
LAYERS = 3
GATES = 3 * P
WS = 64.0
MASKED = -(2.0 ** 62)
EPS = 1e-5
CREDIT = 6
KINDS = 4


def at(g, back=0):
    return g + (1 - back + CREDIT)


ALL = at(NG - 1)
ALLP = at(PAIRS - 1)
DONE = 16 * PAIRS + 16
HALF_DONE = 8 * PAIRS + 16
RW, RI, RH, RL = 0, 2, 5, 8
NRAW = 11


def graph_kernel(nc, x, adj, W0, a0, wl, w_ih, w_hh, b_ih, b_hh, W2, a2, k0, k1, k2, k3, bias3, out):
    with ExitStack() as ctx:
        def sb(name, shape, dt):
            return ctx.enter_context(nc.sbuf_tensor(name, shape, dt))

        def sem(name):
            return ctx.enter_context(nc.semaphore(name))

        def sems(stage, names):
            return {n: sem(f"{stage}_{n}") for n in names.split()}

        X = sb("X", [P, NG, GB, P], F32)
        NP = sb("NP", [P, NG, 2, GW], F16)
        TP = sb("TP", [P, NG, 2, GW], F16)
        HT = sb("HT", [P, NG, GW], F32)
        A1 = sb("A1", [P, NG, GW], F16)
        Z2 = sb("Z2", [P, NG, GW], U8)
        CT = sb("CT", [P, NG, GW], U8)
        WK = sb("WK", [P, 16, GW], F32)
        idf = sb("idf", [P, P], F32)
        idh = sb("idh", [P, P], F16)
        maskI = sb("maskI", [P, P], BF16)
        ones = sb("ones", [P, P], F32)
        half = sb("half", [P, 2 * GB], F32)
        rootp = sb("rootp", [P, 2 * GB], F32)
        nroot = sb("nroot", [P, 2 * GB], F32)
        mhalf = sb("mhalf", [P, 1], F32)
        mone = sb("mone", [P, 1], F32)
        U1 = sb("U1", [P, 2, 2, P], F16)
        U2 = sb("U2", [P, 2, 2, P], F16)
        WR = sb("WR", [P, 2, 2, P], F16)
        CW = sb("CW", [P, LAYERS, 2, GATES], F16)
        HW = sb("HW", [P, 2, GATES], F16)
        acol = sb("acol", [P, 4], F32)
        bcol = sb("bcol", [P, 6], F32)
        brz = sb("brz", [P, 2], F32)
        bhn = sb("bhn", [P, 1], F32)
        kcol = sb("kcol", [P, KINDS], F32)
        bias_all = sb("bias_all", [P, P], F32)
        ksum = sb("ksum", [P, NG], F32)
        kall = sb("kall", [P, 1], F32)
        other = sb("other", [P, 1], I32)
        nmx = sb("nmx", [P, 2 * GB], F32)
        gmx = sb("gmx", [P, 2 * GB], F32)
        den = sb("den", [P, 2 * GB], F32)
        rden = sb("rden", [P, 2 * GB], F32)
        stats = sb("stats", [P, 2, 2 * GB, 6], F32)
        msum = sb("msum", [P, 2, 2 * GB], F32)
        mdif = sb("mdif", [P, 2, 2 * GB], F32)
        mdif2 = sb("mdif2", [P, 2, 2 * GB], F32)
        sq = sb("sq", [P, 2, 2 * GB], F32)
        mean = sb("mean", [P, 2, 2 * GB], F32)
        pvar = sb("pvar", [P, 2, 2 * GB], F32)
        ipow = sb("ipow", [P, 2, 2 * GB], F32)
        rstd = sb("rstd", [P, 2, 2 * GB], F32)
        nrstd = sb("nrstd", [P, 2, 2 * GB], F32)
        shift = sb("shift", [P, 2, 2 * GB], F32)
        PS = ctx.enter_context(nc.psum_tensor("PS", [P, 8, GW], F32))

        prep = NP[:].rearrange("p a s n -> p (a s n)").bitcast(F32)
        raw = prep[:, 0:NRAW * P]
        rawT = prep[:, NRAW * P:2 * NRAW * P]
        abc = prep[:, 2 * NRAW * P:(2 * NRAW + 4) * P]
        zer = prep[:, (2 * NRAW + 4) * P:(2 * NRAW + 5) * P]

        def Z0(g):
            return HT[:, g, 0:GW // 2].bitcast(F16)

        def b4(ap):
            return ap.rearrange("p (b n) -> p b n", b=GB)

        def flat(ap):
            return ap.rearrange("p b n -> p (b n)")

        def cols(b):
            return slice(b * P, (b + 1) * P)

        XS = [[WK[:, 0, :], WK[:, 1, :]], [WK[:, 14, :], WK[:, 15, :]]]
        Y = [[WK[:, 2, :], WK[:, 3, :]], [WK[:, 12, :], WK[:, 13, :]]]
        ADJ = [[WK[:, 4, :], WK[:, 5, :]], [WK[:, 10, :], WK[:, 11, :]]]

        def message(j, u):
            slot = 12 + (j % 2) * 2 + u
            return WK[:, slot, 0:GW // 2].bitcast(F16), WK[:, slot, GW // 2:GW].bitcast(F16)

        s_w = sem("s_w")
        s_id = sem("s_id")
        s_abc = sem("s_abc")
        s_rawT = sem("s_rawT")
        s_rawTc = sem("s_rawTc")
        s_prod = sem("s_prod")
        s_hi = sem("s_hi")
        s_lo = sem("s_lo")
        s_b = sem("s_b")
        s_ksum = sem("s_ksum")
        s_kred = sem("s_kred")
        s_other = sem("s_other")
        def slot_sems(name):
            return [[sem(f"{name}{h}{u}") for u in range(2)] for h in range(2)]

        s_adj = slot_sems("s_adj")
        s_x = slot_sems("s_x")
        s_out = slot_sems("s_out")
        NSMALL = 14
        TAIL = " y bn part mean agg pw rstd norm tr"
        I = sems("in", "a1 z0 z2 cat kt kev kq xs tr xth xtl")
        G0 = sems("g0", "e wh pt pv small leaky gmx nmx exp ptev whev rden xh xl tev ht" + TAIL)
        GR = sems("gr", "q rg zg hn gi tr r z qh ql hh hl t1 t2 n d zd h nev")
        L1 = sems("l1", "sum xth xtl shift z2f ztf" + TAIL)
        G2 = sems("g2", "e wh pt pv small leaky gmx nmx exp ptev whev rden ht ru neg eu relu res" + TAIL)
        L3 = sems("l3", "g e c small lk al pv xb shift xc" + TAIL)
        for S, stage in ((G0, "g0"), (L1, "l1"), (G2, "g2")):
            S["xc"] = slot_sems(f"{stage}_xc")
        L3["xc"] = s_out

        def credit(eng, S, names):
            for n in names.split():
                eng.sem_inc(S[n], CREDIT)

        def pipelined(eng, pairs, lag, body):
            for i in range(lag):
                body(i, lambda k: k <= i)
            with eng.Fori(lag, pairs) as i:
                body(i, lambda k: True)
            for i in range(pairs, pairs + lag):
                body(i, lambda k: i - k < pairs)

        def pipelined2(eng, pairs, lag, body):
            first = lag + lag % 2
            for p in range(first):
                body(p, p % 2, lambda k: k <= p)
            with eng.Fori(first // 2, pairs // 2) as i:
                for h in range(2):
                    body(i * 2 + h, h, lambda k: True)
            for p in range(pairs, pairs + lag):
                body(p, p % 2, lambda k: p - k < pairs)

        def stored(p, h):
            return p * 8 + (16 - 8 * h)

        def gru_pipelined(eng, body):
            n, back = LAYERS * PAIRS, (LAYERS - 1) * PAIRS
            for j in range(2):
                body(j, lambda k: k <= j, j >= 2)
            with eng.Fori(1, back // 2 + 1) as i:
                for h in range(2):
                    body(i * 2 + h, lambda k: True, True)
            with eng.Fori(back // 2 + 1, n // 2) as i:
                for h in range(2):
                    body(i * 2 + h, lambda k: True, False)
            for j in range(n, n + 2):
                body(j, lambda k: j - k < n, False)

        block = ctx.enter_context(nc.Block())

        @block.sync
        def _(eng):
            for S in (G0, L1, G2, L3):
                for h in range(2):
                    for u in range(2):
                        eng.sem_inc(S["xc"][h][u], 16)
            xg = x.rearrange("(g b) n d -> g n b d", b=GB)
            ag = adj.rearrange("(g b) n m -> g n b m", b=GB)
            og = out.rearrange("(g b) n d -> g n b d", b=GB)
            with eng.Fori(0, PAIRS // 2) as i:
                for h in range(2):
                    for u in range(2):
                        g = i * 4 + (2 * h + u)
                        eng.wait_ge(I["a1"], at(g, 4))
                        eng.wait_ge(I["z2"], at(g, 4))
                        eng.wait_ge(I["z0"], at(g, 4))
                        eng.wait_ge(I["cat"], at(g, 4))
                        eng.dma_start(b4(ADJ[h][u]).bitcast(I32), ag[g]).then_inc(s_adj[h][u], 16)
                        eng.wait_ge(I["xs"], at(g, 4))
                        eng.dma_start(X[:, g], xg[g]).then_inc(s_x[h][u], 16)
            for S in (G0, G2):
                with eng.Fori(0, PAIRS) as i:
                    for u in range(2):
                        g = i * 2 + u
                        eng.wait_ge(S["norm"], at(g))
                        eng.dma_start(X[:, g], b4(XS[0][u])).then_inc(S["xc"][0][u], 16)
                if S is G0:
                    with eng.Fori(0, PAIRS // 2) as i:
                        for h in range(2):
                            for u in range(2):
                                g = i * 4 + (2 * h + u)
                                eng.wait_ge(L1["norm"], at(g))
                                eng.dma_start(X[:, g], b4(XS[h][u])).then_inc(L1["xc"][h][u], 16)
            with eng.Fori(0, PAIRS // 2) as i:
                for h in range(2):
                    for u in range(2):
                        g = i * 4 + (2 * h + u)
                        eng.wait_ge(L3["norm"], at(g))
                        eng.dma_start(og[g], b4(XS[h][u])).then_inc(s_out[h][u], 16)
            for S in (L1, L3):
                for h in range(2):
                    for u in range(2):
                        eng.wait_ge(S["xc"][h][u], HALF_DONE)
            for S in (G0, G2):
                for u in range(2):
                    eng.wait_ge(S["xc"][0][u], DONE)

        @block.tensor
        def _(eng):
            def mm(o, lhsT, rhs, start=True, stop=True):
                return eng.matmul(o, lhsT, rhs, start=start, stop=stop, skip_group_check=True)

            def pair_product(o, lh, ll, rh, rl, start=True):
                mm(o, lh, rh, start=start, stop=False)
                mm(o, lh, rl, start=False, stop=False)
                return mm(o, ll, rh, start=False, stop=True)

            def x_transpose(slot, bank):
                for b in range(GB):
                    last = eng.transpose(PS[:, bank, cols(b)], slot[:, cols(b)], idf[:])
                return last

            credit(eng, I, "kt tr")
            credit(eng, G0, "e wh pt pv tr")
            credit(eng, GR, "q rg zg hn gi tr")
            credit(eng, L1, "sum tr")
            credit(eng, G2, "e wh pt pv tr")
            credit(eng, L3, "e pv")

            eng.wait_ge(s_id, 8)
            eng.wait_ge(s_w, 16 * NSMALL)
            for k in range(NRAW):
                last = eng.transpose(PS[:, k // 4, cols(k % 4)], raw[:, cols(k)], idf[:])
            last.then_inc(s_rawT, 1)
            eng.wait_ge(s_rawTc, 1)
            for l in range(LAYERS):
                mm(PS[:, 3 + l, 0:GATES], rawT[:, cols(RL + l)], rawT[:, RI * P:RH * P])
            eng.wait_ge(s_abc, 1)
            for v in range(2):
                mm(PS[:, 6, cols(v)], raw[:, 0:P], abc[:, cols(v)])
            for v in range(2, 4):
                last = mm(PS[:, 6, cols(v)], rawT[:, P:2 * P], abc[:, cols(v)])
            last.then_inc(s_prod, 1)

            eng.wait_ge(s_lo, 6)
            with eng.Fori(0, PAIRS) as i:
                for u in range(2):
                    g = i * 2 + u
                    eng.wait_ge(I["cat"], at(g))
                    eng.wait_ge(I["kev"], at(g, 2))
                    bank = PS[:, u, 0:GW // 2].bitcast(F16)
                    slot = WK[:, 6 + u, 0:GW // 2].bitcast(F16)
                    for b in range(GB):
                        last = eng.transpose(bank[:, cols(b)], slot[:, cols(b)], idh[:])
                    last.then_inc(I["kt"], 1)
                    eng.wait_ge(I["xs"], at(g))
                    eng.wait_ge(I["xtl"], at(g, 2))
                    x_transpose(XS[0][u], 2 + u).then_inc(I["tr"], 1)
            eng.wait_ge(I["kq"], ALL)
            mm(PS[:, 7, 0:NG], ones[:], ksum[:]).then_inc(s_ksum, 1)

            def attention(S, G, masked, evacuated, first):
                lag = 3 if first else 4

                def round_(i, live):
                    if live(0):
                        for u in range(2):
                            g = i * 2 + u
                            eng.wait_ge(S["leaky"], at(g, 2))
                            mm(PS[:, u, :], maskI[:], masked(g), start=True, stop=False)
                            th, tl = TP[:, g, 0, :], TP[:, g, 1, :]
                            pair_product(PS[:, u, :], U2[:, G, 0, :], U2[:, G, 1, :], th, tl, start=False)
                            for b in range(GB):
                                last = pair_product(PS[:, u, cols(b)], TP[:, g, 0, cols(b)], TP[:, g, 1, cols(b)],
                                                    U1[:, G, 0, :], U1[:, G, 1, :], start=False)
                            last.then_inc(S["e"], 1)
                    if live(1):
                        for u in range(2):
                            g = (i - 1) * 2 + u
                            eng.wait_ge(S["exp"], at(g))
                            eng.wait_ge(S["ptev"], at(g, 2))
                            for b in range(GB):
                                last = eng.transpose(PS[:, 4 + u, cols(b)], WK[:, 6 + u, cols(b)], idf[:])
                            last.then_inc(S["pt"], 1)
                    if live(lag):
                        for u in range(2):
                            g = (i - lag) * 2 + u
                            eng.wait_ge(S["whev"], at(g, 2 - 2 * lag) if live(1) else ALL)
                            eng.wait_ge(S[evacuated], at(g, 2))
                            if first:
                                eng.wait_ge(S["xl"], at(g))
                                bank = PS[:, 2 + u, :].bitcast(F16)
                                for s in range(2):
                                    for b in range(GB):
                                        last = eng.transpose(bank[:, s * GW + b * P:s * GW + (b + 1) * P],
                                                             NP[:, g, s, cols(b)], idh[:])
                            else:
                                eng.wait_ge(S["norm"], at(g))
                                last = x_transpose(XS[0][u], 2 + u)
                            last.then_inc(S["tr"], 1)
                    if live(1):
                        for u in range(2):
                            g = (i - 1) * 2 + u
                            eng.wait_ge(S["ptev"], at(g))
                            eng.wait_ge(S["whev"], at(g))
                            eng.wait_ge(S["y" if first else "ru"], at(g, 2))
                            for b in range(GB):
                                last = mm(PS[:, 6 + u, cols(b)], WK[:, 8 + u, cols(b)], WK[:, 10 + u, cols(b)])
                            last.then_inc(S["pv"], 1)
                    if live(0):
                        for u in range(2):
                            g = i * 2 + u
                            eng.wait_ge(S["whev"], at(g, 2))
                            if live(lag):
                                eng.wait_ge(S[evacuated], at(g, 2 * lag))
                            for b in range(GB):
                                last = pair_product(PS[:, 2 + u, cols(b)], TP[:, g, 0, cols(b)], TP[:, g, 1, cols(b)],
                                                    WR[:, G, 0, :], WR[:, G, 1, :])
                            last.then_inc(S["wh"], 1)
                pipelined(eng, PAIRS, lag, round_)

            eng.wait_ge(I["z0"], ALL)
            eng.wait_ge(I["kev"], ALL)
            eng.wait_ge(I["xtl"], ALL)
            attention(G0, 0, Z0, "tev", True)

            eng.wait_ge(G0["ht"], ALL)
            eng.wait_ge(G0["tev"], ALL)
            eng.wait_ge(G0["y"], ALL)
            for u in range(2):
                eng.wait_ge(G0["xc"][0][u], DONE)

            def gru_round(j, live, back):
                for u in range(2):
                    if live(0):
                        t = j * 2 + u
                        g = (j % PAIRS) * 2 + u
                        eng.wait_ge(GR["nev"], at(t, NG) + NG)
                        eng.wait_ge(GR["ql"], at(t, 2))
                        for b in range(GB):
                            mm(PS[:, u, cols(b)], NP[:, g, 0, cols(b)], A1[:, g, cols(b)], start=True, stop=False)
                            last = mm(PS[:, u, cols(b)], NP[:, g, 1, cols(b)], A1[:, g, cols(b)], start=False, stop=True)
                        last.then_inc(GR["q"], 1)
                    if live(1):
                        t = (j - 1) * 2 + u
                        g = ((j - 1) % PAIRS) * 2 + u
                        l = (j - 1) // PAIRS
                        th, tl = TP[:, g, 0, :], TP[:, g, 1, :]
                        qh, ql = message(j - 1, u)

                        def gate(bank, k, state, message):
                            c = cols(k)
                            if state:
                                last = pair_product(PS[:, bank, :], HW[:, 0, c], HW[:, 1, c], th, tl)
                            if message:
                                last = pair_product(PS[:, bank, :], CW[:, l, 0, c], CW[:, l, 1, c], qh, ql, start=not state)
                            return last
                        eng.wait_ge(GR["hl"], at(t, NG) + NG)
                        eng.wait_ge(GR["ql"], at(t))
                        eng.wait_ge(GR["r"], at(t, 1))
                        gate(2, 0, True, True).then_inc(GR["rg"], 1)
                        eng.wait_ge(GR["t1"], at(t, 1))
                        gate(4, 2, True, False).then_inc(GR["hn"], 1)
                        eng.wait_ge(GR["t2"], at(t, 1))
                        gate(5, 2, False, True).then_inc(GR["gi"], 1)
                        eng.wait_ge(GR["z"], at(t, 1))
                        gate(3, 1, True, True).then_inc(GR["zg"], 1)
                    if back:
                        t = (j - 2) * 2 + u
                        g = ((j - 2) % PAIRS) * 2 + u
                        eng.wait_ge(GR["hl"], at(t) + NG)
                        eng.wait_ge(GR["nev"], at(t, 2) + NG)
                        bank = PS[:, 6 + u, :].bitcast(F16)
                        for s in range(2):
                            for b in range(GB):
                                last = eng.transpose(bank[:, s * GW + b * P:s * GW + (b + 1) * P],
                                                     TP[:, g, s, cols(b)], idh[:])
                        last.then_inc(GR["tr"], 1)
            gru_pipelined(eng, gru_round)

            def l1_round(p, h, live):
                if live(0):
                    for u in range(2):
                        g = p * 2 + u
                        eng.wait_ge(GR["hl"], at(g) + LAYERS * NG)
                        eng.wait_ge(L1["y"], at(g, 2))
                        for b in range(GB):
                            mm(PS[:, u, cols(b)], TP[:, g, 0, cols(b)], idh[:], start=True, stop=False)
                            last = mm(PS[:, u, cols(b)], TP[:, g, 1, cols(b)], idh[:], start=False, stop=True)
                        last.then_inc(L1["sum"], 1)
                if live(2):
                    for u in range(2):
                        g = (p - 2) * 2 + u
                        eng.wait_ge(L1["norm"], at(g))
                        eng.wait_ge(L1["xtl"], at(g, 2))
                        x_transpose(XS[h][u], 2 + u).then_inc(L1["tr"], 1)
            pipelined2(eng, PAIRS, 2, l1_round)

            eng.wait_ge(L1["xtl"], ALL)
            eng.wait_ge(L1["z2f"], ALL)
            attention(G2, 1, lambda g: NP[:, g, 0, :], "ht", False)

            eng.wait_ge(G2["ht"], ALL)
            eng.wait_ge(G2["y"], ALL)
            eng.wait_ge(L1["ztf"], ALL)

            def neighbours(g, u, weights):
                eng.wait_ge(L3["al"], at(g))
                eng.wait_ge(L3["y"], at(g, 2))
                for b in range(GB):
                    last = mm(PS[:, 4 + u, cols(b)], weights[:, cols(b)], X[:, g, b, :])
                last.then_inc(L3["pv"], 1)

            def one_kind(p, h, live):
                if live(0):
                    for u in range(2):
                        g = p * 2 + u
                        eng.wait_ge(L3["g"], at(g))
                        eng.wait_ge(L3["lk"], at(g, 2))
                        mm(PS[:, u, :], maskI[:], NP[:, g, 1, :], start=True, stop=False)
                        for b in range(GB):
                            last = mm(PS[:, u, cols(b)], WK[:, 4 + u, cols(b)], HT[:, g, cols(b)], start=False)
                        last.then_inc(L3["e"], 1)
                if live(1):
                    for u in range(2):
                        neighbours((p - 1) * 2 + u, u, WK[:, 10 + u, :])

            def all_kinds(p, h, live):
                for u in range(2):
                    if live(0):
                        g = p * 2 + u
                        eng.wait_ge(L3["g"], at(g))
                        eng.wait_ge(L3["lk"], at(g, 1))
                        for k in range(KINDS):
                            for b in range(GB):
                                last = mm(PS[:, k, cols(b)], WK[:, 4 + k, cols(b)], HT[:, g, cols(b)])
                        last.then_inc(L3["e"], 1)
                        neighbours(g, u, WK[:, 10, :])

            eng.wait_ge(s_other, 1)
            more = eng.value_load(other[0:1, 0:1], min_val=0, max_val=1)
            with eng.If(more == 0):
                pipelined2(eng, PAIRS, 1, one_kind)
            with eng.Else():
                pipelined2(eng, PAIRS, 0, all_kinds)

        @block.scalar
        def _(eng):
            small = [(raw[:, 0:P], W0), (raw[:, P:2 * P], W2),
                     (raw[:, RI * P:RH * P].rearrange("p (c d) -> p c d", c=3), w_ih.rearrange("(c p) d -> p c d", p=P)),
                     (raw[:, RH * P:RL * P].rearrange("p (c d) -> p c d", c=3), w_hh.rearrange("(c p) d -> p c d", p=P)),
                     (raw[:, RL * P:NRAW * P].rearrange("p (c d) -> p c d", c=3), wl.rearrange("l p d -> p l d")),
                     (acol[:, 0:2], a0.rearrange("(c p) -> p c", p=P)), (acol[:, 2:4], a2.rearrange("(c p) -> p c", p=P)),
                     (bcol[:, 0:3], b_ih.rearrange("(c p) -> p c", p=P)), (bcol[:, 3:6], b_hh.rearrange("(c p) -> p c", p=P))]
            small += [(kcol[:, k:k + 1], v) for k, v in enumerate((k0, k1, k2, k3))]
            small += [(bias_all[:], bias3.rearrange("(a d) -> a d", a=1).to_broadcast([P, P]))]
            assert len(small) == NSMALL
            for dst, src in small:
                eng.dma_start(dst, src, allow_slow_non_contiguous=True).then_inc(s_w, 16)
            credit(eng, I, "cat xth kq")
            credit(eng, G0, "small exp ptev whev xh tev")
            credit(eng, GR, "r z qh hh n")
            credit(eng, L1, "xth ztf norm")
            credit(eng, G2, "small exp ptev ru eu ht")
            credit(eng, L3, "small al norm")
            eng.preload_act_table(ACT.Exp)

            def copy(o, i, scale=1.0):
                return eng.activation(o, i, ACT.Copy, scale=scale)

            eng.wait_ge(s_rawT, 1)
            copy(rawT[:, 0:NRAW * P], PS[:, 0:3, :].rearrange("p a b -> p (a b)")[:, 0:NRAW * P]).then_inc(s_rawTc, 1)
            eng.wait_ge(s_rawTc, 1)
            copy(WR[:, 0, 0, :], rawT[:, 0:P], WS).then_inc(s_hi, 1)
            copy(WR[:, 1, 0, :], raw[:, P:2 * P], WS).then_inc(s_hi, 1)
            copy(HW[:, 0, :], rawT[:, RH * P:RL * P], WS).then_inc(s_hi, 1)
            eng.wait_ge(s_prod, 1)
            copy(CW[:, :, 0, :], PS[:, 3:6, 0:GATES], WS).then_inc(s_hi, 1)
            prod = PS[:, 6, :].rearrange("p (g v n) -> p g v n", g=2, v=2)
            copy(U1[:, :, 0, :], prod[:, :, 0, :], WS).then_inc(s_hi, 1)
            copy(U2[:, :, 0, :], prod[:, :, 1, :], WS).then_inc(s_hi, 1)

            eng.wait_ge(s_id, 8)

            def in_round(p, h, live):
                if live(0):
                    for u in range(2):
                        g = p * 2 + u
                        eng.wait_ge(s_adj[h][u], stored(p, h))
                        eng.wait_ge(I["kt"], at(g, 2))
                        copy(WK[:, 6 + u, 0:GW // 2].bitcast(F16), ADJ[h][u].bitcast(I32)).then_inc(I["cat"], 1)
                if live(1):
                    for u in range(2):
                        g = (p - 1) * 2 + u
                        eng.wait_ge(I["tr"], at(g))
                        copy(TP[:, g, 0, :], PS[:, 2 + u, :]).then_inc(I["xth"], 1)
                    for u in range(2):
                        g = (p - 1) * 2 + u
                        eng.wait_ge(I["kev"], at(g))
                        eng.wait_ge(I["kq"], at(g, 2))
                        eng.activation(WK[:, 8 + u, :], CT[:, g, :], ACT.Square, bias=mhalf[:, 0:1],
                                       accum_out=ksum[:, bass.ds(g, 1)]).then_inc(I["kq"], 1)
            pipelined2(eng, PAIRS, 1, in_round)

            def attention(S, first):
                def round_(i, live):
                    if live(0):
                        for u in range(2):
                            g = i * 2 + u
                            eng.wait_ge(S["e"], at(g))
                            eng.wait_ge(S["gmx"], at(g, 2))
                            eng.wait_ge(S["exp"], at(g, 2))
                            copy(WK[:, 4 + u, :], PS[:, u, :], 0.2).then_inc(S["small"], 1)
                    if live(1):
                        for u in range(2):
                            g = (i - 1) * 2 + u
                            eng.wait_ge(S["pt"], at(g))
                            eng.wait_ge(S["pv"], at(g, 2))
                            copy(WK[:, 8 + u, :], PS[:, 4 + u, :]).then_inc(S["ptev"], 1)
                    if not first and live(4):
                        for u in range(2):
                            g = (i - 4) * 2 + u
                            eng.wait_ge(S["tr"], at(g))
                            copy(HT[:, g, :], PS[:, 2 + u, :]).then_inc(S["ht"], 1)
                    if first and live(3):
                        for u in range(2):
                            g = (i - 3) * 2 + u
                            eng.wait_ge(S["tr"], at(g))
                            copy(TP[:, g].rearrange("p s n -> p (s n)"), PS[:, 2 + u, :].bitcast(F16)).then_inc(S["tev"], 1)
                    if not first and live(2):
                        for u in range(2):
                            g = (i - 2) * 2 + u
                            eng.wait_ge(S["relu"], at(g))
                            eng.activation(WK[:, 14 + u, :], WK[:, 14 + u, :], ACT.Exp).then_inc(S["eu"], 1)
                    if live(0):
                        eng.wait_ge(S["nmx"], at(i))
                        eng.wait_ge(S["rden"], at(i, 1))
                        for u in range(2):
                            g = i * 2 + u
                            eng.wait_ge(S["pt"], at(g, 2))
                            for b in range(GB):
                                k = u * GB + b
                                last = eng.activation(WK[:, 6 + u, cols(b)], WK[:, 4 + u, cols(b)], ACT.Exp,
                                                      bias=nmx[:, k:k + 1], scale=1.0 / WS, accum_out=den[:, k:k + 1])
                            last.then_inc(S["exp"], 1)
                    if first and live(2):
                        for u in range(2):
                            g = (i - 2) * 2 + u
                            eng.wait_ge(S["norm"], at(g))
                            copy(NP[:, g, 0, :], XS[0][u]).then_inc(S["xh"], 1)
                    if first and live(0):
                        for u in range(2):
                            g = i * 2 + u
                            eng.wait_ge(S["wh"], at(g))
                            eng.wait_ge(S["pv"], at(g, 2))
                            copy(WK[:, 10 + u, :], PS[:, 2 + u, :], 1.0 / WS).then_inc(S["whev"], 1)
                    if not first and live(1):
                        eng.wait_ge(S["rden"], at(i - 1))
                        for u in range(2):
                            g = (i - 1) * 2 + u
                            eng.wait_ge(S["pv"], at(g))
                            eng.wait_ge(S["y"], at(g, 2))
                            for b in range(GB):
                                k = u * GB + b
                                last = eng.activation(WK[:, 12 + u, cols(b)], PS[:, 6 + u, cols(b)], ACT.Identity,
                                                      scale=rden[:, k:k + 1])
                            last.then_inc(S["ru"], 1)
                pipelined(eng, PAIRS, 3 if first else 4, round_)

            attention(G0, True)

            eng.preload_act_table(ACT.Sigmoid)

            def gru_round(j, live):
                for u in range(2):
                    if live(0):
                        t = j * 2 + u
                        eng.wait_ge(GR["q"], at(t))
                        eng.wait_ge(GR["zg"], at(t, 4))
                        copy(message(j, u)[0], PS[:, u, :]).then_inc(GR["qh"], 1)
                    if live(1):
                        t = (j - 1) * 2 + u
                        eng.wait_ge(GR["rg"], at(t))
                        eng.wait_ge(GR["t1"], at(t, 2))
                        eng.activation(WK[:, 2 + u, :], PS[:, 2, :], ACT.Sigmoid, bias=brz[:, 0:1], scale=1.0 / WS).then_inc(GR["r"], 1)
                    if live(1):
                        t = (j - 1) * 2 + u
                        eng.wait_ge(GR["t2"], at(t))
                        eng.wait_ge(GR["h"], at(t, 2))
                        eng.activation(WK[:, 6 + u, :], WK[:, 8 + u, :], ACT.Tanh, bias=bcol[:, 2:3], scale=1.0 / WS).then_inc(GR["n"], 1)
                    if live(2 - u):
                        t = (j - 1) * 2 + u - 1
                        g = ((j - 2 + u) % PAIRS) * 2 + (1 - u)
                        eng.wait_ge(GR["h"], at(t))
                        copy(TP[:, g, 0, :], HT[:, g, :]).then_inc(GR["hh"], 1)
                    if live(1):
                        t = (j - 1) * 2 + u
                        eng.wait_ge(GR["zg"], at(t))
                        eng.wait_ge(GR["zd"], at(t, 2))
                        eng.activation(WK[:, 4 + u, :], PS[:, 3, :], ACT.Sigmoid, bias=brz[:, 1:2], scale=1.0 / WS).then_inc(GR["z"], 1)
            pipelined(eng, LAYERS * PAIRS, 2, gru_round)

            def norm(S, p, h):
                eng.wait_ge(S["shift"], at(p))
                for u in range(2):
                    eng.wait_ge(S["xc"][h][u], stored(p, h))
                    for b in range(GB):
                        k = u * GB + b
                        last = eng.activation(XS[h][u][:, cols(b)], Y[h][u][:, cols(b)], ACT.Identity,
                                              bias=shift[:, h, k:k + 1], scale=rstd[:, h, k:k + 1])
                    last.then_inc(S["norm"], 1)

            def l1_round(p, h, live):
                if live(2):
                    for u in range(2):
                        g = (p - 2) * 2 + u
                        eng.wait_ge(L1["tr"], at(g))
                        copy(TP[:, g, 0, :], PS[:, 2 + u, :]).then_inc(L1["xth"], 1)
                if live(1):
                    eng.wait_ge(L1["tr"], at(p * 2 - 1, 4))
                    norm(L1, p - 1, 1 - h)
                if live(0):
                    for u in range(2):
                        g = p * 2 + u
                        eng.wait_ge(L1["sum"], at(g))
                        eng.activation(NP[:, g, 1, :], CT[:, g, :], ACT.Square, bias=mone[:, 0:1]).then_inc(L1["ztf"], 1)
            pipelined2(eng, PAIRS, 2, l1_round)

            eng.preload_act_table(ACT.Exp)
            attention(G2, False)
            eng.preload_act_table(ACT.Sigmoid)

            def edge_weights(g, scores, weights, used):
                eng.wait_ge(L3["lk"], at(g))
                eng.wait_ge(L3["pv"], at(g, used))
                eng.activation(weights, scores, ACT.Sigmoid).then_inc(L3["al"], 1)

            def one_kind(p, h, live):
                if live(0):
                    for u in range(2):
                        g = p * 2 + u
                        eng.wait_ge(L3["e"], at(g))
                        eng.wait_ge(L3["al"], at(g, 2))
                        copy(WK[:, 6 + u, :], PS[:, u, :], 0.2).then_inc(L3["small"], 1)
                if live(2):
                    norm(L3, p - 2, h)
                if live(0):
                    for u in range(2):
                        edge_weights(p * 2 + u, WK[:, 6 + u, :], WK[:, 10 + u, :], 2)

            def all_kinds(p, h, live):
                if live(0):
                    for u in range(2):
                        edge_weights(p * 2 + u, WK[:, 10, :], WK[:, 10, :], 1)
                if live(1):
                    norm(L3, p - 1, 1 - h)

            for u in range(2):
                eng.wait_ge(G2["xc"][0][u], DONE)
            eng.wait_ge(s_other, 1)
            more = eng.value_load(other[0:1, 0:1], min_val=0, max_val=1)
            with eng.If(more == 0):
                eng.preload_act_table(ACT.Sigmoid)
                pipelined2(eng, PAIRS, 2, one_kind)
            with eng.Else():
                eng.preload_act_table(ACT.Sigmoid)
                pipelined2(eng, PAIRS, 1, all_kinds)

        @block.vector
        def _(eng):
            def stt(o, a, s, b, op0, op1):
                return eng.scalar_tensor_tensor(out=o, in0=a, scalar=s, in1=b, op0=op0, op1=op1)

            tt = eng.tensor_tensor

            def ln_sums(S, p, h):
                for u in range(2):
                    eng.wait_ge(S["y"], at(p * 2 + u))
                    for b in range(GB):
                        last = eng.bn_stats(stats[:, h, u * GB + b, :], Y[h][u][:, cols(b)])
                last.then_inc(S["bn"], 1)

            def ln_parts(S, p, h):
                even_mean, even_sq, odd_mean, odd_sq = (stats[:, h, :, k] for k in (1, 2, 4, 5))
                eng.wait_ge(S["bn"], at(p))
                tt(mdif[:, h, :], even_mean, odd_mean, ALU.subtract)
                tt(msum[:, h, :], even_mean, odd_mean, ALU.add)
                tt(sq[:, h, :], even_sq, odd_sq, ALU.add).then_inc(S["part"], 1)

            def ln_square(S, p, h):
                eng.wait_ge(S["part"], at(p))
                stt(mdif2[:, h, :], mdif[:, h, :], P / 4.0, mdif[:, h, :], ALU.mult, ALU.mult)
                eng.tensor_scalar(mean[:, h, :], msum[:, h, :], 0.5, None, ALU.mult).then_inc(S["mean"], 1)

            def ln_total(S, p, h):
                eng.wait_ge(S["mean"], at(p))
                stt(pvar[:, h, :], sq[:, h, :], P * EPS, mdif2[:, h, :], ALU.add, ALU.add).then_inc(S["agg"], 1)

            def ln_stats(S, p, h):
                for part in (ln_sums, ln_parts, ln_square, ln_total):
                    part(S, p, h)

            def ln_norm(S, i):
                eng.wait_ge(S["rstd"], at(i))
                for u in range(2):
                    eng.wait_ge(S["xc"][0][u], i * 16 + 16)
                    for b in range(GB):
                        k = u * GB + b
                        last = eng.tensor_scalar(XS[0][u][:, cols(b)], Y[0][u][:, cols(b)], mean[:, 0, k:k + 1],
                                                 rstd[:, 0, k:k + 1], ALU.subtract, ALU.mult)
                    last.then_inc(S["norm"], 1)

            credit(eng, I, "a1 z2 z0 kev xtl")
            credit(eng, G0, "leaky gmx nmx rden y bn part mean agg norm")
            credit(eng, GR, "t1 t2 h ql hl nev")
            credit(eng, L1, "y bn part mean agg xtl z2f")
            credit(eng, G2, "leaky gmx nmx rden whev neg y bn part mean agg norm")
            credit(eng, L3, "g c lk y bn part mean agg")
            eng.sem_inc(GR["hl"], NG)
            eng.sem_inc(GR["nev"], NG)

            eng.memset(zer, 0.0).then_inc(s_b, 1)
            eng.wait_ge(s_w, 16 * NSMALL)
            eng.wait_ge(s_b, 1)
            for v in range(4):
                last = eng.tensor_scalar(abc[:, cols(v)], zer, acol[:, v:v + 1], None, ALU.add)
            last.then_inc(s_abc, 1)
            tt(brz[:], bcol[:, 0:2], bcol[:, 3:5], ALU.add).then_inc(s_b, 1)
            eng.tensor_scalar(bhn[:], bcol[:, 5:6], WS, None, ALU.mult).then_inc(s_b, 1)
            eng.wait_ge(s_hi, 3)
            stt(WR[:, 0, 1, :], rawT[:, 0:P], WS, WR[:, 0, 0, :], ALU.mult, ALU.subtract).then_inc(s_lo, 1)
            stt(WR[:, 1, 1, :], raw[:, P:2 * P], WS, WR[:, 1, 0, :], ALU.mult, ALU.subtract).then_inc(s_lo, 1)
            stt(HW[:, 1, :], rawT[:, RH * P:RL * P], WS, HW[:, 0, :], ALU.mult, ALU.subtract).then_inc(s_lo, 1)
            eng.wait_ge(s_hi, 6)
            stt(CW[:, :, 1, :], PS[:, 3:6, 0:GATES], WS, CW[:, :, 0, :], ALU.mult, ALU.subtract).then_inc(s_lo, 1)
            prod = PS[:, 6, :].rearrange("p (g v n) -> p g v n", g=2, v=2)
            stt(U1[:, :, 1, :], prod[:, :, 0, :], WS, U1[:, :, 0, :], ALU.mult, ALU.subtract).then_inc(s_lo, 1)
            stt(U2[:, :, 1, :], prod[:, :, 1, :], WS, U2[:, :, 0, :], ALU.mult, ALU.subtract).then_inc(s_lo, 1)

            def in_round(p, h, live):
                if live(0):
                    for u in range(2):
                        g = p * 2 + u
                        a = ADJ[h][u].bitcast(I32)
                        eng.wait_ge(s_adj[h][u], stored(p, h))
                        eng.tensor_scalar(A1[:, g, :], a, 0.0, None, ALU.not_equal).then_inc(I["a1"], 1)
                        eng.tensor_scalar(Z2[:, g, :], a, 0.0, None, ALU.is_le).then_inc(I["z2"], 1)
                        eng.tensor_scalar(Z0(g), a, 0.0, None, ALU.is_equal).then_inc(I["z0"], 1)
                if live(1):
                    for u in range(2):
                        g = (p - 1) * 2 + u
                        eng.wait_ge(I["kt"], at(g))
                        eng.tensor_scalar(CT[:, g, :], PS[:, u, 0:GW // 2].bitcast(F16), KINDS + 1.0, 0.0, ALU.min, ALU.max).then_inc(I["kev"], 1)
                    for u in range(2):
                        g = (p - 1) * 2 + u
                        eng.wait_ge(I["xth"], at(g))
                        tt(TP[:, g, 1, :], PS[:, 2 + u, :], TP[:, g, 0, :], ALU.subtract).then_inc(I["xtl"], 1)
            pipelined2(eng, PAIRS, 1, in_round)

            eng.wait_ge(s_ksum, 1)
            eng.tensor_reduce(kall[:], PS[:, 7, 0:NG], AX.X, ALU.add).then_inc(s_kred, 1)
            eng.wait_ge(s_kred, 1)
            eng.tensor_scalar(other[:], kall[:], 0.25 * B * P * P, None, ALU.is_gt).then_inc(s_other, 1)

            def attention(S, first):
                def round_(i, live):
                    if live(0):
                        for u in range(2):
                            g = i * 2 + u
                            eng.wait_ge(S["small"], at(g))
                            eng.wait_ge(S["exp"], at(g, 2))
                            tt(WK[:, 4 + u, :], PS[:, u, :], WK[:, 4 + u, :], ALU.max).then_inc(S["leaky"], 1)
                        for u in range(2):
                            g = i * 2 + u
                            eng.wait_ge(S["leaky"], at(g))
                            eng.tensor_reduce(gmx[:, u * GB:(u + 1) * GB], b4(WK[:, 4 + u, :]), AX.X, ALU.max).then_inc(S["gmx"], 1)
                    if live(1):
                        eng.wait_ge(S["exp"], at(i * 2 - 1))
                        eng.reciprocal(rden[:], den[:]).then_inc(S["rden"], 1)
                    if live(0):
                        eng.wait_ge(S["gmx"], at(i * 2 + 1))
                        eng.tensor_scalar(nmx[:], gmx[:], -1.0 / WS, None, ALU.mult).then_inc(S["nmx"], 1)
                    if first:
                        if live(2):
                            eng.wait_ge(S["xl"], at((i - 2) * 2 + 1, 2))
                            ln_norm(S, i - 2)
                        if live(1):
                            eng.wait_ge(S["rden"], at(i - 1))
                            for u in range(2):
                                g = (i - 1) * 2 + u
                                eng.wait_ge(S["pv"], at(g))
                                eng.wait_ge(S["norm"], at(g, 2))
                                for b in range(GB):
                                    k = u * GB + b
                                    last = stt(Y[0][u][:, cols(b)], PS[:, 6 + u, cols(b)], rden[:, k:k + 1], X[:, g, b, :], ALU.mult, ALU.add)
                                last.then_inc(S["y"], 1)
                            ln_stats(S, i - 1, 0)
                    else:
                        if live(0):
                            for u in range(2):
                                g = i * 2 + u
                                eng.wait_ge(S["wh"], at(g))
                                eng.wait_ge(S["pv"], at(g, 2))
                                eng.tensor_scalar(WK[:, 10 + u, :], PS[:, 2 + u, :], 1.0 / WS, None, ALU.mult).then_inc(S["whev"], 1)
                        if live(3):
                            eng.wait_ge(S["tr"], at((i - 3) * 2 + 1, 2))
                            ln_norm(S, i - 3)
                        if live(2):
                            for u in range(2):
                                g = (i - 2) * 2 + u
                                eng.wait_ge(S["eu"], at(g))
                                eng.wait_ge(S["res"], at(g))
                                eng.wait_ge(S["norm"], at(g, 2))
                                stt(Y[0][u], WK[:, 14 + u, :], -1.0, WK[:, 12 + u, :], ALU.add, ALU.add).then_inc(S["y"], 1)
                            ln_stats(S, i - 2, 0)
                        if live(1):
                            for u in range(2):
                                g = (i - 1) * 2 + u
                                eng.wait_ge(S["ru"], at(g))
                                eng.tensor_scalar(WK[:, 14 + u, :], WK[:, 12 + u, :], 0.0, None, ALU.min).then_inc(S["neg"], 1)
                pipelined(eng, PAIRS, 3, round_)

            eng.wait_ge(I["tr"], ALL)
            attention(G0, True)

            def gru_round(j, live, back):
                for u in range(2):
                    if live(0):
                        t = j * 2 + u
                        eng.wait_ge(GR["qh"], at(t))
                        qh, ql = message(j, u)
                        tt(ql, PS[:, u, :], qh, ALU.subtract).then_inc(GR["ql"], 1)
                    if live(1):
                        t = (j - 1) * 2 + u
                        eng.wait_ge(GR["r"], at(t))
                        eng.wait_ge(GR["hn"], at(t))
                        eng.wait_ge(GR["n"], at(t, 2))
                        stt(WK[:, 8 + u, :], PS[:, 4, :], bhn[:, 0:1], WK[:, 2 + u, :], ALU.add, ALU.mult).then_inc(GR["t1"], 1)
                        eng.wait_ge(GR["t1"], at(t))
                        eng.wait_ge(GR["gi"], at(t))
                        tt(WK[:, 8 + u, :], PS[:, 5, :], WK[:, 8 + u, :], ALU.add).then_inc(GR["t2"], 1)
                    if live(2 - u):
                        t = (j - 1) * 2 + u - 1
                        g = ((j - 2 + u) % PAIRS) * 2 + (1 - u)
                        eng.wait_ge(GR["zd"], at(t))
                        tt(HT[:, g, :], WK[:, 6 + (1 - u), :], WK[:, 10 + (1 - u), :], ALU.add).then_inc(GR["h"], 1)
                    if back:
                        t = (j - 2) * 2 + u
                        g = ((j - 2) % PAIRS) * 2 + u
                        eng.wait_ge(GR["tr"], at(t))
                        eng.tensor_copy(NP[:, g].rearrange("p s n -> p (s n)"), PS[:, 6 + u, :].bitcast(F16)).then_inc(GR["nev"], 1)
                    if live(2 - u):
                        t = (j - 1) * 2 + u - 1
                        g = ((j - 2 + u) % PAIRS) * 2 + (1 - u)
                        eng.wait_ge(GR["hh"], at(t))
                        tt(TP[:, g, 1, :], HT[:, g, :], TP[:, g, 0, :], ALU.subtract).then_inc(GR["hl"], 1)
            gru_pipelined(eng, gru_round)

            def l1_round(p, h, live):
                if live(0):
                    for u in range(2):
                        g = p * 2 + u
                        eng.wait_ge(L1["sum"], at(g))
                        eng.wait_ge(L1["norm"], at(g, 4))
                        tt(Y[h][u], PS[:, u, :], flat(X[:, g]), ALU.add).then_inc(L1["y"], 1)
                    ln_sums(L1, p, h)
                    for u in range(2):
                        g = p * 2 + u
                        eng.tensor_copy(NP[:, g, 0, :], Z2[:, g, :]).then_inc(L1["z2f"], 1)
                    for part in (ln_parts, ln_square, ln_total):
                        part(L1, p, h)
                if live(2):
                    for u in range(2):
                        g = (p - 2) * 2 + u
                        eng.wait_ge(L1["xth"], at(g))
                        tt(TP[:, g, 1, :], PS[:, 2 + u, :], TP[:, g, 0, :], ALU.subtract).then_inc(L1["xtl"], 1)
            pipelined2(eng, PAIRS, 2, l1_round)

            for h in range(2):
                for u in range(2):
                    eng.wait_ge(L1["xc"][h][u], HALF_DONE)
            attention(G2, False)

            eng.wait_ge(G2["ht"], ALL)
            eng.wait_ge(G2["tr"], ALL)
            for u in range(2):
                eng.wait_ge(G2["xc"][0][u], DONE)

            def sums(p, h):
                for u in range(2):
                    g = p * 2 + u
                    eng.wait_ge(L3["xb"], at(g))
                    eng.wait_ge(L3["pv"], at(g))
                    eng.wait_ge(L3["norm"], at(g, 4))
                    tt(Y[h][u], PS[:, 4 + u, :], WK[:, 8 + u, :], ALU.add).then_inc(L3["y"], 1)
                ln_stats(L3, p, h)

            def one_kind(p, h, live):
                if live(1):
                    for u in range(2):
                        g = (p - 1) * 2 + u
                        eng.wait_ge(L3["small"], at(g))
                        tt(WK[:, 6 + u, :], PS[:, u, :], WK[:, 6 + u, :], ALU.max).then_inc(L3["lk"], 1)
                if live(0):
                    for u in range(2):
                        g = p * 2 + u
                        eng.wait_ge(L3["e"], at(g, 2))
                        eng.tensor_scalar(WK[:, 4 + u, :], HT[:, g, :], kcol[:, 0:1], None, ALU.mult).then_inc(L3["g"], 1)
                if live(2):
                    sums(p - 2, h)

            def all_kinds(p, h, live):
                if live(0):
                    for u in range(2):
                        g = p * 2 + u
                        eng.wait_ge(L3["e"], at(g, 1))
                        for k in range(KINDS):
                            last = eng.tensor_scalar(WK[:, 4 + k, :], HT[:, g, :], kcol[:, k:k + 1], None, ALU.mult)
                        last.then_inc(L3["g"], 1)
                        sc, tmp, kinds = WK[:, 10, :], WK[:, 11, :], CT[:, g, :]
                        eng.wait_ge(L3["e"], at(g))
                        eng.wait_ge(L3["pv"], at(g, 1))
                        steps = 2 * KINDS + 3
                        done = g * steps + CREDIT
                        stt(sc, kinds, 1.0, PS[:, 0, :], ALU.is_equal, ALU.mult).then_inc(L3["c"], 1)
                        for k in range(1, KINDS):
                            stt(tmp, kinds, k + 1.0, PS[:, k, :], ALU.is_equal, ALU.mult).then_inc(L3["c"], 1)
                            eng.wait_ge(L3["c"], done + (2 * k))
                            tt(sc, sc, tmp, ALU.add).then_inc(L3["c"], 1)
                            eng.wait_ge(L3["c"], done + (2 * k + 1))
                        for n, k in enumerate((0.0, KINDS + 1.0)):
                            eng.tensor_scalar(tmp, kinds, k, MASKED, ALU.is_equal, ALU.mult).then_inc(L3["c"], 1)
                            eng.wait_ge(L3["c"], done + (2 * KINDS + 2 * n))
                            tt(sc, sc, tmp, ALU.add).then_inc(L3["c"], 1)
                            eng.wait_ge(L3["c"], done + (2 * KINDS + 2 * n + 1))
                        stt(sc, sc, 0.2, sc, ALU.mult, ALU.max).then_inc(L3["lk"], 1)
                    sums(p, h)

            more = eng.value_load(other[0:1, 0:1], min_val=0, max_val=1)
            with eng.If(more == 0):
                pipelined2(eng, PAIRS, 2, one_kind)
            with eng.Else():
                pipelined2(eng, PAIRS, 0, all_kinds)

        @block.gpsimd
        def _(eng):
            tt = eng.tensor_tensor
            eng.memset(idf[:], 0.0).then_inc(s_id, 1)
            eng.memset(idh[:], 0.0).then_inc(s_id, 1)
            eng.memset(maskI[:], 0.0).then_inc(s_id, 1)
            eng.memset(rootp[:], float(P) ** 0.5)
            eng.memset(nroot[:], -float(P) ** 0.5)
            eng.memset(mhalf[:], -0.5)
            eng.memset(mone[:], -1.0)
            eng.memset(ones[:], 1.0).then_inc(s_id, 1)
            eng.memset(half[:], -0.5).then_inc(s_id, 1)
            eng.wait_ge(s_id, 5)
            for m, v in ((idf, 1.0), (idh, 1.0), (maskI, MASKED)):
                eng.affine_select(out=m[:], in_=m[:], compare_op=ALU.not_equal, fill=v, base=0,
                                  pattern=[[-1, P]], channel_multiplier=1).then_inc(s_id, 1)
            credit(eng, I, "xs")
            credit(eng, G0, "pw rstd xl ht")
            credit(eng, GR, "d zd")
            credit(eng, L1, "pw rstd shift")
            credit(eng, G2, "pw rstd relu res")
            credit(eng, L3, "xb pw rstd shift")

            with eng.Fori(0, PAIRS // 2) as i:
                for h in range(2):
                    for u in range(2):
                        g = i * 4 + (2 * h + u)
                        eng.wait_ge(s_x[h][u], i * 16 + 16)
                        eng.wait_ge(I["tr"], at(g, 2))
                        eng.tensor_copy(XS[0][u], flat(X[:, g])).then_inc(I["xs"], 1)

            def ln_rstd(S, p, h, shifted=False):
                eng.wait_ge(S["agg"], at(p))
                tt(ipow[:, h, :], pvar[:, h, :], half[:], ALU.pow).then_inc(S["pw"], 1)
                eng.wait_ge(S["pw"], at(p))
                if shifted:
                    tt(nrstd[:, h, :], ipow[:, h, :], nroot[:], ALU.mult)
                tt(rstd[:, h, :], ipow[:, h, :], rootp[:], ALU.mult).then_inc(S["rstd"], 1)
                if shifted:
                    eng.wait_ge(S["rstd"], at(p))
                    tt(shift[:, h, :], mean[:, h, :], nrstd[:, h, :], ALU.mult).then_inc(S["shift"], 1)

            def first_round(i, live):
                if live(3):
                    for u in range(2):
                        g = (i - 3) * 2 + u
                        eng.wait_ge(G0["tev"], at(g))
                        tt(HT[:, g, :], TP[:, g, 0, :], TP[:, g, 1, :], ALU.add).then_inc(G0["ht"], 1)
                if live(2):
                    for u in range(2):
                        g = (i - 2) * 2 + u
                        eng.wait_ge(G0["xh"], at(g))
                        tt(NP[:, g, 1, :], XS[0][u], NP[:, g, 0, :], ALU.subtract).then_inc(G0["xl"], 1)
                if live(1):
                    ln_rstd(G0, i - 1, 0)
            pipelined(eng, PAIRS, 3, first_round)

            with eng.Fori(0, LAYERS * PAIRS) as j:
                for u in range(2):
                    t = j * 2 + u
                    g = (j % PAIRS) * 2 + u
                    eng.wait_ge(GR["n"], at(t))
                    eng.wait_ge(GR["h"], at(t, 2))
                    tt(WK[:, 10 + u, :], HT[:, g, :], WK[:, 6 + u, :], ALU.subtract).then_inc(GR["d"], 1)
                    eng.wait_ge(GR["d"], at(t))
                    eng.wait_ge(GR["z"], at(t))
                    tt(WK[:, 10 + u, :], WK[:, 10 + u, :], WK[:, 4 + u, :], ALU.mult).then_inc(GR["zd"], 1)

            with eng.Fori(0, PAIRS // 2) as i:
                for h in range(2):
                    ln_rstd(L1, i * 2 + h, h, shifted=True)

            def third_round(i, live):
                if live(2):
                    ln_rstd(G2, i - 2, 0)
                if live(1):
                    for u in range(2):
                        g = (i - 1) * 2 + u
                        eng.wait_ge(G2["neg"], at(g))
                        tt(WK[:, 12 + u, :], WK[:, 12 + u, :], WK[:, 14 + u, :], ALU.subtract).then_inc(G2["relu"], 1)
                    for u in range(2):
                        g = (i - 1) * 2 + u
                        eng.wait_ge(G2["relu"], at(g))
                        tt(WK[:, 12 + u, :], WK[:, 12 + u, :], flat(X[:, g]), ALU.add).then_inc(G2["res"], 1)
            pipelined(eng, PAIRS, 2, third_round)

            eng.wait_ge(G2["norm"], ALL)
            eng.wait_ge(G2["pv"], ALL)
            for u in range(2):
                eng.wait_ge(G2["xc"][0][u], DONE)

            def last_round(p, h, live):
                if live(0):
                    for u in range(2):
                        g = p * 2 + u
                        eng.wait_ge(L3["y"], at(g, 2))
                        tt(b4(WK[:, 8 + u, :]), X[:, g], bias_all[:, None, :].to_broadcast([P, GB, P]), ALU.add).then_inc(L3["xb"], 1)
                if live(1):
                    ln_rstd(L3, p - 1, 1 - h, shifted=True)
            pipelined2(eng, PAIRS, 1, last_round)


_INS = ['x', 'adj', 'L0_gnn_W', 'L0_gnn_a', 'L1_gnn_weight', 'L1_gnn_w_ih', 'L1_gnn_w_hh', 'L1_gnn_b_ih', 'L1_gnn_b_hh',
        'L2_gnn_W', 'L2_gnn_a', 'L3_gnn_a0', 'L3_gnn_a1', 'L3_gnn_a2', 'L3_gnn_a3', 'L3_gnn_bias']
_OUTS = [((B, P, P), 'float32')]


def kernel(**inputs):
    import numpy as _np
    import concourse.bacc as _bacc
    from concourse import mybir as _mybir
    from concourse.bass_utils import run_bass_kernel_spmd as _run

    nc = _bacc.Bacc("TRN2", target_bir_lowering=False, num_devices=1)
    arrays, args = {}, []
    for name in _INS:
        a = _np.ascontiguousarray(inputs[name])
        arrays[f"in_{name}_dram"] = a
        args.append(nc.dram_tensor(f"in_{name}_dram", a.shape, _mybir.dt.from_np(a.dtype), kind="ExternalInput").ap())
    for i, (shape, dtype) in enumerate(_OUTS):
        dt = _mybir.dt.from_np(_np.dtype(dtype))
        args.append(nc.dram_tensor(f"out_{i}_dram", shape, dt, kind="ExternalOutput").ap())
    graph_kernel(nc, *args)
    r = _run(nc, [arrays], core_ids=[0])
    return r.results[0]["out_0_dram"]
```

```python
from contextlib import ExitStack

import concourse.bass as bass
from concourse import mybir

F32 = mybir.dt.float32
F16 = mybir.dt.float16
BF16 = mybir.dt.bfloat16
U8 = mybir.dt.uint8
I32 = mybir.dt.int32
ALU = mybir.AluOpType
ACT = mybir.ActivationFunctionType
AX = mybir.AxisListType

P = 128
B = 64
GB = 4
NG = B // GB
PAIRS = NG // 2
GW = GB * P
LAYERS = 3
GATES = 3 * P
WS = 64.0
MASKED = -(2.0 ** 62)
EPS = 1e-5
CREDIT = 6
KINDS = 4


def at(g, back=0):
    return g + (1 - back + CREDIT)


LAST_ROUND = (LAYERS - 1) * PAIRS + 2
ALL = at(NG - 1)
ALLP = at(PAIRS - 1)
DONE = 16 * PAIRS + 16
HALF_DONE = 8 * PAIRS + 16
RW, RI, RH, RL = 0, 2, 5, 8
NRAW = 11


def graph_kernel(nc, x, adj, W0, a0, wl, w_ih, w_hh, b_ih, b_hh, W2, a2, k0, k1, k2, k3, bias3, out):
    with ExitStack() as ctx:
        def sb(name, shape, dt):
            return ctx.enter_context(nc.sbuf_tensor(name, shape, dt))

        def sem(name):
            return ctx.enter_context(nc.semaphore(name))

        def sems(stage, names):
            return {n: sem(f"{stage}_{n}") for n in names.split()}

        X = sb("X", [P, NG, GB, P], F32)
        NP = sb("NP", [P, NG, 2, GW], F16)
        TP = sb("TP", [P, NG, 2, GW], F16)
        HT = sb("HT", [P, NG, GW], F32)
        A1 = sb("A1", [P, NG, GW], F16)
        Z2 = sb("Z2", [P, NG, GW], U8)
        CT = sb("CT", [P, NG, GW], U8)
        WK = sb("WK", [P, 16, GW], F32)
        idf = sb("idf", [P, P], F32)
        idh = sb("idh", [P, P], F16)
        maskI = sb("maskI", [P, P], BF16)
        ones = sb("ones", [P, P], F32)
        half = sb("half", [P, 2 * GB], F32)
        rootp = sb("rootp", [P, 2 * GB], F32)
        nroot = sb("nroot", [P, 2 * GB], F32)
        mhalf = sb("mhalf", [P, 1], F32)
        mone = sb("mone", [P, 1], F32)
        U1 = sb("U1", [P, 2, 2, P], F16)
        U2 = sb("U2", [P, 2, 2, P], F16)
        WR = sb("WR", [P, 2, 2, P], F16)
        CW = sb("CW", [P, LAYERS, 2, GATES], F16)
        HW = sb("HW", [P, 2, GATES], F16)
        acol = sb("acol", [P, 4], F32)
        bcol = sb("bcol", [P, 6], F32)
        brz = sb("brz", [P, 2], F32)
        bhn = sb("bhn", [P, 1], F32)
        kcol = sb("kcol", [P, KINDS], F32)
        bias_all = sb("bias_all", [P, P], F32)
        ksum = sb("ksum", [P, NG], F32)
        kall = sb("kall", [P, 1], F32)
        other = sb("other", [P, 1], I32)
        nmx = sb("nmx", [P, 2 * GB], F32)
        gmx = sb("gmx", [P, 2 * GB], F32)
        den = sb("den", [P, 2 * GB], F32)
        rden = sb("rden", [P, 2 * GB], F32)
        stats = sb("stats", [P, 2, 2 * GB, 6], F32)
        msum = sb("msum", [P, 2, 2 * GB], F32)
        mdif = sb("mdif", [P, 2, 2 * GB], F32)
        mdif2 = sb("mdif2", [P, 2, 2 * GB], F32)
        sq = sb("sq", [P, 2, 2 * GB], F32)
        mean = sb("mean", [P, 2, 2 * GB], F32)
        pvar = sb("pvar", [P, 2, 2 * GB], F32)
        ipow = sb("ipow", [P, 2, 2 * GB], F32)
        rstd = sb("rstd", [P, 2, 2 * GB], F32)
        nrstd = sb("nrstd", [P, 2, 2 * GB], F32)
        shift = sb("shift", [P, 2, 2 * GB], F32)
        PS = ctx.enter_context(nc.psum_tensor("PS", [P, 8, GW], F32))

        prep = NP[:].rearrange("p a s n -> p (a s n)").bitcast(F32)
        raw = prep[:, 0:NRAW * P]
        rawT = prep[:, NRAW * P:2 * NRAW * P]
        abc = prep[:, 2 * NRAW * P:(2 * NRAW + 4) * P]
        zer = prep[:, (2 * NRAW + 4) * P:(2 * NRAW + 5) * P]

        def Z0(g):
            return HT[:, g, 0:GW // 2].bitcast(F16)

        def b4(ap):
            return ap.rearrange("p (b n) -> p b n", b=GB)

        def flat(ap):
            return ap.rearrange("p b n -> p (b n)")

        def cols(b):
            return slice(b * P, (b + 1) * P)

        XS = [[WK[:, 0, :], WK[:, 1, :]], [WK[:, 14, :], WK[:, 15, :]]]
        Y = [[WK[:, 2, :], WK[:, 3, :]], [WK[:, 12, :], WK[:, 13, :]]]

        def ln_slots(S, h):
            return (XS[1 - h], Y[1 - h]) if S is L3 else (XS[h], Y[h])

        def second_new(h, u):
            return WK[:, 2 * h + u, :]

        ADJ = [[WK[:, 4, :], WK[:, 5, :]], [WK[:, 10, :], WK[:, 11, :]]]

        def message(j, u):
            slot = 12 + (j % 2) * 2 + u
            return WK[:, slot, 0:GW // 2].bitcast(F16), WK[:, slot, GW // 2:GW].bitcast(F16)

        s_w = sem("s_w")
        s_id = sem("s_id")
        s_abc = sem("s_abc")
        s_rawT = sem("s_rawT")
        s_rawTc = sem("s_rawTc")
        s_prod = sem("s_prod")
        s_hi = sem("s_hi")
        s_lo = sem("s_lo")
        s_b = sem("s_b")
        s_ksum = sem("s_ksum")
        s_kred = sem("s_kred")
        s_other = sem("s_other")
        def slot_sems(name):
            return [[sem(f"{name}{h}{u}") for u in range(2)] for h in range(2)]

        s_adj = slot_sems("s_adj")
        s_x = slot_sems("s_x")
        s_out = slot_sems("s_out")
        NSMALL = 14
        TAIL = " y bn part mean agg pw rstd norm tr"
        I = sems("in", "a1 z0 z2 cat kt kev xs tr xth xtl")
        G0 = sems("g0", "e wh pt pv small leaky gmx nmx exp ptev whev rden xh xl tev ht" + TAIL)
        GR = sems("gr", "kq q rg zg hn gi tr r z qh ql hh hl t1 t2 n d zd h nev")
        L1 = sems("l1", "sum xth xtl shift z2f ztf" + TAIL)
        G2 = sems("g2", "e wh pt pv small leaky gmx nmx exp ptev whev rden ht ru neg eu relu res" + TAIL)
        L3 = sems("l3", "g e c small lk al pv xb shift xc" + TAIL)
        for S, stage in ((G0, "g0"), (L1, "l1"), (G2, "g2")):
            S["xc"] = slot_sems(f"{stage}_xc")
        L3["xc"] = s_out

        def credit(eng, S, names):
            for n in names.split():
                eng.sem_inc(S[n], CREDIT)

        def filled(eng, pairs, lag, body):
            first = lag + lag % 2
            for i in range(first):
                body(i, lambda k: k <= i)
            with eng.Fori(first // 2, pairs // 2) as i:
                for h in range(2):
                    body(i * 2 + h, lambda k: True)

        def drained(pairs, lag, body, between=()):
            for i in range(pairs, pairs + lag):
                body(i, lambda k: i - k < pairs)
                if i - pairs < len(between):
                    between[i - pairs]()

        def pipelined(eng, pairs, lag, body, between=()):
            filled(eng, pairs, lag, body)
            drained(pairs, lag, body, between)

        def pipelined2(eng, pairs, lag, body, start=0):
            first = lag + lag % 2
            for p in range(start, first):
                body(p, p % 2, lambda k: k <= p)
            with eng.Fori(first // 2, pairs // 2) as i:
                for h in range(2):
                    body(i * 2 + h, h, lambda k: True)
            for p in range(pairs, pairs + lag):
                body(p, p % 2, lambda k: p - k < pairs)

        def early(body, lag, p):
            assert p < lag + lag % 2
            return lambda: body(p, p % 2, lambda k: k <= p)

        def stored(p, h):
            return p * 8 + (16 - 8 * h)

        def gru_pipelined(eng, body, norm_step):
            n, last = LAYERS * PAIRS, LAST_ROUND

            def with_norm(j, h, live, started):
                body(j, live, False, lambda u, *part: norm_step(j - last, h, u, started, *part))

            with eng.Fori(1, PAIRS // 2 + 1) as i:
                for h in range(2):
                    body(i * 2 + h, lambda k: True, True, kinds=True)
            with eng.Fori(PAIRS // 2 + 1, last // 2) as i:
                for h in range(2):
                    body(i * 2 + h, lambda k: True, True)
            for j in range(last, last + 2):
                with_norm(j, j % 2, lambda k: True, lambda k: k <= j - last)
            with eng.Fori(last // 2 + 1, n // 2) as i:
                for h in range(2):
                    with_norm(i * 2 + h, h, lambda k: True, lambda k: True)
            for j in range(n, n + 2):
                with_norm(j, j % 2, lambda k: j - k < n, lambda k: True)
            for p in range(PAIRS, PAIRS + 2):
                for u in range(2):
                    norm_step(p, p % 2, u, lambda k: p - k < PAIRS)

        def gru_first(body):
            return [lambda j=j: body(j, lambda k: k <= j, False) for j in range(2)]

        block = ctx.enter_context(nc.Block())

        @block.sync
        def _(eng):
            for S in (G0, L1, G2, L3):
                for h in range(2):
                    for u in range(2):
                        eng.sem_inc(S["xc"][h][u], 16)
            xg = x.rearrange("(g b) n d -> g n b d", b=GB)
            ag = adj.rearrange("(g b) n m -> g n b m", b=GB)
            og = out.rearrange("(g b) n d -> g n b d", b=GB)
            with eng.Fori(0, PAIRS // 2) as i:
                for h in range(2):
                    for u in range(2):
                        g = i * 4 + (2 * h + u)
                        eng.wait_ge(I["a1"], at(g, 4))
                        eng.wait_ge(I["z2"], at(g, 4))
                        eng.wait_ge(I["cat"], at(g, 4))
                        eng.dma_start(b4(ADJ[h][u]).bitcast(I32), ag[g]).then_inc(s_adj[h][u], 16)
                        eng.wait_ge(I["xs"], at(g, 4))
                        eng.dma_start(X[:, g], xg[g]).then_inc(s_x[h][u], 16)
            for S in (G0, G2):
                with eng.Fori(0, PAIRS) as i:
                    for u in range(2):
                        g = i * 2 + u
                        eng.wait_ge(S["norm"], at(g))
                        eng.dma_start(X[:, g], b4(XS[0][u])).then_inc(S["xc"][0][u], 16)
                if S is G0:
                    with eng.Fori(0, PAIRS // 2) as i:
                        for h in range(2):
                            for u in range(2):
                                g = i * 4 + (2 * h + u)
                                eng.wait_ge(L1["norm"], at(g))
                                eng.dma_start(X[:, g], b4(second_new(h, u))).then_inc(L1["xc"][h][u], 16)
            with eng.Fori(0, PAIRS // 2) as i:
                for h in range(2):
                    for u in range(2):
                        g = i * 4 + (2 * h + u)
                        eng.wait_ge(L3["norm"], at(g))
                        eng.dma_start(og[g], b4(ln_slots(L3, h)[0][u])).then_inc(s_out[h][u], 16)
            for S in (L1, L3):
                for h in range(2):
                    for u in range(2):
                        eng.wait_ge(S["xc"][h][u], HALF_DONE)
            for S in (G0, G2):
                for u in range(2):
                    eng.wait_ge(S["xc"][0][u], DONE)

        @block.tensor
        def _(eng):
            def mm(o, lhsT, rhs, start=True, stop=True):
                return eng.matmul(o, lhsT, rhs, start=start, stop=stop, skip_group_check=True)

            def pair_product(o, lh, ll, rh, rl, start=True):
                mm(o, lh, rh, start=start, stop=False)
                mm(o, lh, rl, start=False, stop=False)
                return mm(o, ll, rh, start=False, stop=True)

            def x_transpose(slot, bank):
                for b in range(GB):
                    last = eng.transpose(PS[:, bank, cols(b)], slot[:, cols(b)], idf[:])
                return last

            credit(eng, I, "kt tr")
            credit(eng, G0, "e wh pt pv tr")
            credit(eng, GR, "q rg zg hn gi tr")
            credit(eng, L1, "sum tr")
            credit(eng, G2, "e wh pt pv tr")
            credit(eng, L3, "e pv")

            eng.wait_ge(s_id, 8)
            eng.wait_ge(s_w, 16 * NSMALL)
            for k in range(NRAW):
                last = eng.transpose(PS[:, k // 4, cols(k % 4)], raw[:, cols(k)], idf[:])
            last.then_inc(s_rawT, 1)
            eng.wait_ge(s_rawTc, 1)
            for l in range(LAYERS):
                mm(PS[:, 3 + l, 0:GATES], rawT[:, cols(RL + l)], rawT[:, RI * P:RH * P])
            eng.wait_ge(s_abc, 1)
            for v in range(2):
                mm(PS[:, 6, cols(v)], raw[:, 0:P], abc[:, cols(v)])
            for v in range(2, 4):
                last = mm(PS[:, 6, cols(v)], rawT[:, P:2 * P], abc[:, cols(v)])
            last.then_inc(s_prod, 1)

            eng.wait_ge(s_lo, 6)
            with eng.Fori(0, PAIRS) as i:
                for u in range(2):
                    g = i * 2 + u
                    eng.wait_ge(I["cat"], at(g))
                    eng.wait_ge(I["kev"], at(g, 2))
                    bank = PS[:, u, 0:GW // 2].bitcast(F16)
                    slot = WK[:, 6 + u, 0:GW // 2].bitcast(F16)
                    for b in range(GB):
                        last = eng.transpose(bank[:, cols(b)], slot[:, cols(b)], idh[:])
                    last.then_inc(I["kt"], 1)
                    eng.wait_ge(I["xs"], at(g))
                    eng.wait_ge(I["xtl"], at(g, 2))
                    x_transpose(XS[0][u], 2 + u).then_inc(I["tr"], 1)

            def attention(S, G, masked, evacuated, first):
                lag = 3 if first else 4

                def round_(i, live):
                    if live(0):
                        for u in range(2):
                            g = i * 2 + u
                            eng.wait_ge(S["leaky"], at(g, 2))
                            mm(PS[:, u, :], maskI[:], masked(g), start=True, stop=False)
                            th, tl = TP[:, g, 0, :], TP[:, g, 1, :]
                            pair_product(PS[:, u, :], U2[:, G, 0, :], U2[:, G, 1, :], th, tl, start=False)
                            for b in range(GB):
                                last = pair_product(PS[:, u, cols(b)], TP[:, g, 0, cols(b)], TP[:, g, 1, cols(b)],
                                                    U1[:, G, 0, :], U1[:, G, 1, :], start=False)
                            last.then_inc(S["e"], 1)
                    if live(1):
                        for u in range(2):
                            g = (i - 1) * 2 + u
                            eng.wait_ge(S["exp"], at(g))
                            eng.wait_ge(S["ptev"], at(g, 2))
                            for b in range(GB):
                                last = eng.transpose(PS[:, 4 + u, cols(b)], WK[:, 6 + u, cols(b)], idf[:])
                            last.then_inc(S["pt"], 1)
                    if live(lag):
                        for u in range(2):
                            g = (i - lag) * 2 + u
                            eng.wait_ge(S["whev"], at(g, 2 - 2 * lag) if live(1) else ALL)
                            eng.wait_ge(S[evacuated], at(g, 2))
                            if first:
                                eng.wait_ge(S["xl"], at(g))
                                bank = PS[:, 2 + u, :].bitcast(F16)
                                for s in range(2):
                                    for b in range(GB):
                                        last = eng.transpose(bank[:, s * GW + b * P:s * GW + (b + 1) * P],
                                                             NP[:, g, s, cols(b)], idh[:])
                            else:
                                eng.wait_ge(S["norm"], at(g))
                                last = x_transpose(XS[0][u], 2 + u)
                            last.then_inc(S["tr"], 1)
                    if live(1):
                        for u in range(2):
                            g = (i - 1) * 2 + u
                            eng.wait_ge(S["ptev"], at(g))
                            eng.wait_ge(S["whev"], at(g))
                            eng.wait_ge(S["y" if first else "ru"], at(g, 2))
                            for b in range(GB):
                                last = mm(PS[:, 6 + u, cols(b)], WK[:, 8 + u, cols(b)], WK[:, 10 + u, cols(b)])
                            last.then_inc(S["pv"], 1)
                    if live(0):
                        for u in range(2):
                            g = i * 2 + u
                            eng.wait_ge(S["whev"], at(g, 2))
                            if live(lag):
                                eng.wait_ge(S[evacuated], at(g, 2 * lag))
                            for b in range(GB):
                                last = pair_product(PS[:, 2 + u, cols(b)], TP[:, g, 0, cols(b)], TP[:, g, 1, cols(b)],
                                                    WR[:, G, 0, :], WR[:, G, 1, :])
                            last.then_inc(S["wh"], 1)
                return round_

            def gru_round(j, live, back, norm_part=None, kinds=False):
                for u in range(2):
                    if live(0):
                        t = j * 2 + u
                        g = (j % PAIRS) * 2 + u
                        eng.wait_ge(GR["nev"], at(t, NG) + NG)
                        eng.wait_ge(GR["ql"], at(t, 2))
                        for b in range(GB):
                            mm(PS[:, u, cols(b)], NP[:, g, 0, cols(b)], A1[:, g, cols(b)], start=True, stop=False)
                            last = mm(PS[:, u, cols(b)], NP[:, g, 1, cols(b)], A1[:, g, cols(b)], start=False, stop=True)
                        last.then_inc(GR["q"], 1)
                    if live(1):
                        t = (j - 1) * 2 + u
                        g = ((j - 1) % PAIRS) * 2 + u
                        l = (j - 1) // PAIRS
                        th, tl = TP[:, g, 0, :], TP[:, g, 1, :]
                        qh, ql = message(j - 1, u)

                        def gate(bank, k, state, message):
                            c = cols(k)
                            if state:
                                last = pair_product(PS[:, bank, :], HW[:, 0, c], HW[:, 1, c], th, tl)
                            if message:
                                last = pair_product(PS[:, bank, :], CW[:, l, 0, c], CW[:, l, 1, c], qh, ql, start=not state)
                            return last
                        eng.wait_ge(GR["hl"], at(t, NG) + NG)
                        eng.wait_ge(GR["ql"], at(t))
                        eng.wait_ge(GR["r"], at(t, 1))
                        gate(4, 0, True, True).then_inc(GR["rg"], 1)
                        eng.wait_ge(GR["t1"], at(t, 1))
                        gate(6, 2, True, False).then_inc(GR["hn"], 1)
                        eng.wait_ge(GR["t2"], at(t, 1))
                        gate(7, 2, False, True).then_inc(GR["gi"], 1)
                    if norm_part:
                        norm_part(u)
                    if live(1):
                        eng.wait_ge(GR["z"], at(t, 1))
                        gate(5, 1, True, True).then_inc(GR["zg"], 1)
                    if back:
                        t = (j - 2) * 2 + u
                        g = ((j - 2) % PAIRS) * 2 + u
                        eng.wait_ge(GR["hl"], at(t) + NG)
                        eng.wait_ge(GR["nev"], at(t, 2) + NG)
                        bank = PS[:, 2 + u, :].bitcast(F16)
                        for s in range(2):
                            for b in range(GB):
                                last = eng.transpose(bank[:, s * GW + b * P:s * GW + (b + 1) * P],
                                                     TP[:, g, s, cols(b)], idh[:])
                        last.then_inc(GR["tr"], 1)
            def norm_step(p, h, u, live):
                if live(2):
                    g = (p - 2) * 2 + u
                    eng.wait_ge(L1["norm"], at(g))
                    eng.wait_ge(L1["xtl"], at(g, 1))
                    x_transpose(second_new(h, u), 3).then_inc(L1["tr"], 1)
                if live(0):
                    g = p * 2 + u
                    if not live(1):
                        eng.wait_ge(GR["nev"], at(2 * NG - 1) + NG)
                    eng.wait_ge(GR["hl"], at(g) + LAYERS * NG)
                    eng.wait_ge(L1["y"], at(g, 1))
                    for b in range(GB):
                        mm(PS[:, 2, cols(b)], TP[:, g, 0, cols(b)], idh[:], start=True, stop=False)
                        last = mm(PS[:, 2, cols(b)], TP[:, g, 1, cols(b)], idh[:], start=False, stop=True)
                    last.then_inc(L1["sum"], 1)

            def gru_1():
                eng.wait_ge(G0["y"], ALL)
                eng.wait_ge(G0["tev"], at(3))
                gru_first(gru_round)[1]()

            def gru_0():
                eng.wait_ge(G0["leaky"], ALL)
                gru_first(gru_round)[0]()

            eng.wait_ge(I["z0"], ALL)
            eng.wait_ge(I["kev"], ALL)
            eng.wait_ge(I["xtl"], ALL)
            pipelined(eng, PAIRS, 3, attention(G0, 0, Z0, "tev", True), (gru_0, gru_1))
            eng.wait_ge(G0["tev"], ALL)
            gru_pipelined(eng, gru_round, norm_step)

            eng.wait_ge(L1["z2f"], ALL)
            eng.wait_ge(L1["xtl"], ALL)
            eng.wait_ge(GR["kq"], ALL)
            mm(PS[:, 7, 0:NG], ones[:], ksum[:]).then_inc(s_ksum, 1)

            third_round = attention(G2, 1, lambda g: NP[:, g, 0, :], "ht", False)
            filled(eng, PAIRS, 4, third_round)


            def neighbours(g, u, weights):
                eng.wait_ge(L3["al"], at(g))
                eng.wait_ge(L3["y"], at(g, 2))
                for b in range(GB):
                    last = mm(PS[:, 4 + u, cols(b)], weights[:, cols(b)], X[:, g, b, :])
                last.then_inc(L3["pv"], 1)

            def one_kind(p, h, live):
                if live(0):
                    for u in range(2):
                        g = p * 2 + u
                        eng.wait_ge(L3["g"], at(g))
                        eng.wait_ge(L3["lk"], at(g, 2))
                        mm(PS[:, u, :], maskI[:], NP[:, g, 1, :], start=True, stop=False)
                        for b in range(GB):
                            last = mm(PS[:, u, cols(b)], WK[:, 4 + u, cols(b)], HT[:, g, cols(b)], start=False)
                        last.then_inc(L3["e"], 1)
                if live(1):
                    for u in range(2):
                        neighbours((p - 1) * 2 + u, u, WK[:, 10 + u, :])

            def all_kinds(p, h, live):
                for u in range(2):
                    if live(0):
                        g = p * 2 + u
                        eng.wait_ge(L3["g"], at(g))
                        eng.wait_ge(L3["lk"], at(g, 1))
                        for k in range(KINDS):
                            for b in range(GB):
                                last = mm(PS[:, k, cols(b)], WK[:, 4 + k, cols(b)], HT[:, g, cols(b)])
                        last.then_inc(L3["e"], 1)
                        neighbours(g, u, WK[:, 10, :])

            def last_0():
                eng.wait_ge(G2["leaky"], ALL)
                eng.wait_ge(L1["ztf"], ALL)
                early(one_kind, 1, 0)()

            def last_1():
                for u in range(2):
                    eng.wait_ge(G2["xc"][0][u], 16 * 2 + 16)
                early(one_kind, 1, 1)()

            eng.wait_ge(s_other, 1)
            more = eng.value_load(other[0:1, 0:1], min_val=0, max_val=1)
            with eng.If(more == 0):
                drained(PAIRS, 4, third_round, (lambda: None, last_0, last_1))
                for u in range(2):
                    eng.wait_ge(G2["xc"][0][u], DONE)
                pipelined2(eng, PAIRS, 1, one_kind, 2)
            with eng.Else():
                drained(PAIRS, 4, third_round)
                eng.wait_ge(G2["ht"], ALL)
                eng.wait_ge(G2["y"], ALL)
                for u in range(2):
                    eng.wait_ge(G2["xc"][0][u], DONE)
                pipelined2(eng, PAIRS, 0, all_kinds)

        @block.scalar
        def _(eng):
            small = [(raw[:, 0:P], W0), (raw[:, P:2 * P], W2),
                     (raw[:, RI * P:RH * P].rearrange("p (c d) -> p c d", c=3), w_ih.rearrange("(c p) d -> p c d", p=P)),
                     (raw[:, RH * P:RL * P].rearrange("p (c d) -> p c d", c=3), w_hh.rearrange("(c p) d -> p c d", p=P)),
                     (raw[:, RL * P:NRAW * P].rearrange("p (c d) -> p c d", c=3), wl.rearrange("l p d -> p l d")),
                     (acol[:, 0:2], a0.rearrange("(c p) -> p c", p=P)), (acol[:, 2:4], a2.rearrange("(c p) -> p c", p=P)),
                     (bcol[:, 0:3], b_ih.rearrange("(c p) -> p c", p=P)), (bcol[:, 3:6], b_hh.rearrange("(c p) -> p c", p=P))]
            small += [(kcol[:, k:k + 1], v) for k, v in enumerate((k0, k1, k2, k3))]
            small += [(bias_all[:], bias3.rearrange("(a d) -> a d", a=1).to_broadcast([P, P]))]
            assert len(small) == NSMALL
            for dst, src in small:
                eng.dma_start(dst, src, allow_slow_non_contiguous=True).then_inc(s_w, 16)
            credit(eng, I, "cat xth z0")
            credit(eng, G0, "small exp ptev whev xh tev")
            credit(eng, GR, "r z qh hh n kq")
            credit(eng, L1, "xth ztf norm")
            credit(eng, G2, "small exp ptev ru eu ht")
            credit(eng, L3, "small al norm")
            eng.preload_act_table(ACT.Exp)

            def copy(o, i, scale=1.0):
                return eng.activation(o, i, ACT.Copy, scale=scale)

            eng.wait_ge(s_rawT, 1)
            copy(rawT[:, 0:NRAW * P], PS[:, 0:3, :].rearrange("p a b -> p (a b)")[:, 0:NRAW * P]).then_inc(s_rawTc, 1)
            eng.wait_ge(s_rawTc, 1)
            copy(WR[:, 0, 0, :], rawT[:, 0:P], WS).then_inc(s_hi, 1)
            copy(WR[:, 1, 0, :], raw[:, P:2 * P], WS).then_inc(s_hi, 1)
            copy(HW[:, 0, :], rawT[:, RH * P:RL * P], WS).then_inc(s_hi, 1)
            eng.wait_ge(s_prod, 1)
            copy(CW[:, :, 0, :], PS[:, 3:6, 0:GATES], WS).then_inc(s_hi, 1)
            prod = PS[:, 6, :].rearrange("p (g v n) -> p g v n", g=2, v=2)
            copy(U1[:, :, 0, :], prod[:, :, 0, :], WS).then_inc(s_hi, 1)
            copy(U2[:, :, 0, :], prod[:, :, 1, :], WS).then_inc(s_hi, 1)

            eng.wait_ge(s_id, 8)

            def in_round(p, h, live):
                if live(0):
                    for u in range(2):
                        g = p * 2 + u
                        eng.wait_ge(s_adj[h][u], stored(p, h))
                        eng.wait_ge(I["kt"], at(g, 2))
                        copy(WK[:, 6 + u, 0:GW // 2].bitcast(F16), ADJ[h][u].bitcast(I32)).then_inc(I["cat"], 1)
                if live(1):
                    for u in range(2):
                        g = (p - 1) * 2 + u
                        eng.wait_ge(I["tr"], at(g))
                        copy(TP[:, g, 0, :], PS[:, 2 + u, :]).then_inc(I["xth"], 1)
                    for u in range(2):
                        g = (p - 1) * 2 + u
                        eng.wait_ge(I["a1"], at(g))
                        eng.activation(Z0(g), A1[:, g, :], ACT.Copy, bias=1.0, scale=-1.0).then_inc(I["z0"], 1)
            pipelined2(eng, PAIRS, 1, in_round)

            def attention(S, first):
                def round_(i, live):
                    if live(0):
                        for u in range(2):
                            g = i * 2 + u
                            eng.wait_ge(S["e"], at(g))
                            eng.wait_ge(S["gmx"], at(g, 2))
                            eng.wait_ge(S["exp"], at(g, 2))
                            copy(WK[:, 4 + u, :], PS[:, u, :], 0.2).then_inc(S["small"], 1)
                    if live(1):
                        for u in range(2):
                            g = (i - 1) * 2 + u
                            eng.wait_ge(S["pt"], at(g))
                            eng.wait_ge(S["pv"], at(g, 2))
                            copy(WK[:, 8 + u, :], PS[:, 4 + u, :]).then_inc(S["ptev"], 1)
                    if not first and live(4):
                        for u in range(2):
                            g = (i - 4) * 2 + u
                            eng.wait_ge(S["tr"], at(g))
                            copy(HT[:, g, :], PS[:, 2 + u, :]).then_inc(S["ht"], 1)
                    if first and live(3):
                        for u in range(2):
                            g = (i - 3) * 2 + u
                            eng.wait_ge(S["tr"], at(g))
                            copy(TP[:, g].rearrange("p s n -> p (s n)"), PS[:, 2 + u, :].bitcast(F16)).then_inc(S["tev"], 1)
                    if not first and live(2):
                        for u in range(2):
                            g = (i - 2) * 2 + u
                            eng.wait_ge(S["relu"], at(g))
                            eng.activation(WK[:, 14 + u, :], WK[:, 14 + u, :], ACT.Exp).then_inc(S["eu"], 1)
                    if live(0):
                        eng.wait_ge(S["nmx"], at(i))
                        eng.wait_ge(S["rden"], at(i, 1))
                        for u in range(2):
                            g = i * 2 + u
                            eng.wait_ge(S["pt"], at(g, 2))
                            for b in range(GB):
                                k = u * GB + b
                                last = eng.activation(WK[:, 6 + u, cols(b)], WK[:, 4 + u, cols(b)], ACT.Exp,
                                                      bias=nmx[:, k:k + 1], scale=1.0 / WS, accum_out=den[:, k:k + 1])
                            last.then_inc(S["exp"], 1)
                    if first and live(2):
                        for u in range(2):
                            g = (i - 2) * 2 + u
                            eng.wait_ge(S["norm"], at(g))
                            copy(NP[:, g, 0, :], XS[0][u]).then_inc(S["xh"], 1)
                    if first and live(0):
                        for u in range(2):
                            g = i * 2 + u
                            eng.wait_ge(S["wh"], at(g))
                            eng.wait_ge(S["pv"], at(g, 2))
                            copy(WK[:, 10 + u, :], PS[:, 2 + u, :], 1.0 / WS).then_inc(S["whev"], 1)
                    if not first and live(1):
                        eng.wait_ge(S["rden"], at(i - 1))
                        for u in range(2):
                            g = (i - 1) * 2 + u
                            eng.wait_ge(S["pv"], at(g))
                            eng.wait_ge(S["y"], at(g, 2))
                            for b in range(GB):
                                k = u * GB + b
                                last = eng.activation(WK[:, 12 + u, cols(b)], PS[:, 6 + u, cols(b)], ACT.Identity,
                                                      scale=rden[:, k:k + 1])
                            last.then_inc(S["ru"], 1)
                return round_

            def state_hi(j, u):
                t = (j - 1) * 2 + u - 1
                g = ((j - 2 + u) % PAIRS) * 2 + (1 - u)
                eng.wait_ge(GR["h"], at(t))
                copy(TP[:, g, 0, :], HT[:, g, :]).then_inc(GR["hh"], 1)

            def gru_round(j, live, back, norm_part=None, kinds=False):
                for u in range(2):
                    if live(0):
                        t = j * 2 + u
                        eng.wait_ge(GR["q"], at(t))
                        eng.wait_ge(GR["zg"], at(t, 4))
                        copy(message(j, u)[0], PS[:, u, :]).then_inc(GR["qh"], 1)
                    if live(1):
                        t = (j - 1) * 2 + u
                        eng.wait_ge(GR["rg"], at(t))
                        eng.wait_ge(GR["n"], at(t, 2))
                        eng.activation(WK[:, 8 + u, :], PS[:, 4, :], ACT.Sigmoid, bias=brz[:, 0:1], scale=1.0 / WS).then_inc(GR["r"], 1)
                    if kinds:
                        g = (j - 2) * 2 + u
                        eng.wait_ge(GR["h"], at((j - 1) * 2 + u, 2))
                        eng.activation(WK[:, 6 + u, :], CT[:, g, :], ACT.Square, bias=mhalf[:, 0:1],
                                       accum_out=ksum[:, bass.ds(g, 1)]).then_inc(GR["kq"], 1)
                    if norm_part:
                        norm_part(u)
                        if live(2 - u):
                            state_hi(j, u)
                    if live(1):
                        t = (j - 1) * 2 + u
                        eng.wait_ge(GR["t2"], at(t))
                        eng.wait_ge(GR["h"], at(t, 2))
                        if kinds:
                            eng.wait_ge(GR["kq"], at((j - 2) * 2 + u))
                        eng.activation(WK[:, 6 + u, :], WK[:, 8 + u, :], ACT.Tanh, bias=bcol[:, 2:3], scale=1.0 / WS).then_inc(GR["n"], 1)
                    if live(2 - u) and not norm_part:
                        state_hi(j, u)
                    if live(1):
                        t = (j - 1) * 2 + u
                        eng.wait_ge(GR["zg"], at(t))
                        eng.wait_ge(GR["zd"], at(t, 2))
                        eng.activation(WK[:, 4 + u, :], PS[:, 5, :], ACT.Sigmoid, bias=brz[:, 1:2], scale=1.0 / WS).then_inc(GR["z"], 1)

            def norm_step(p, h, u, live):
                behind, v, parity = (1, 0, 1 - h) if u else (2, 1, h)
                n = p - behind

                def hi_part():
                    g = (p - 2) * 2 + u
                    eng.wait_ge(L1["tr"], at(g))
                    copy(TP[:, g, 0, :], PS[:, 3, :]).then_inc(L1["xth"], 1)

                draining = not live(0)
                if live(2) and not draining:
                    hi_part()
                if live(behind):
                    eng.wait_ge(L1["shift"], at(n))
                    eng.wait_ge(L1["tr"], at(n * 2 + v, 4))
                    eng.wait_ge(L1["xc"][parity][v], stored(n, parity))
                if live(0):
                    g = p * 2 + u
                    eng.wait_ge(L1["sum"], at(g))
                    eng.activation(NP[:, g, 1, :], CT[:, g, :], ACT.Square, bias=mone[:, 0:1]).then_inc(L1["ztf"], 1)
                if live(behind):
                    g = n * 2 + v
                    for b in range(GB):
                        k = v * GB + b
                        last = eng.activation(second_new(parity, v)[:, cols(b)], HT[:, g, cols(b)], ACT.Identity,
                                              bias=shift[:, parity, k:k + 1], scale=rstd[:, parity, k:k + 1])
                    last.then_inc(L1["norm"], 1)
                if live(2) and draining:
                    hi_part()

            def gru_0():
                eng.preload_act_table(ACT.Sigmoid)
                gru_first(gru_round)[0]()

            pipelined(eng, PAIRS, 3, attention(G0, True), (gru_0, gru_first(gru_round)[1]))
            gru_pipelined(eng, gru_round, norm_step)

            def norm(S, p, h):
                new, y = ln_slots(S, h)
                eng.wait_ge(S["shift"], at(p))
                for u in range(2):
                    eng.wait_ge(S["xc"][h][u], stored(p, h))
                    for b in range(GB):
                        k = u * GB + b
                        last = eng.activation(new[u][:, cols(b)], y[u][:, cols(b)], ACT.Identity,
                                              bias=shift[:, h, k:k + 1], scale=rstd[:, h, k:k + 1])
                    last.then_inc(S["norm"], 1)

            eng.preload_act_table(ACT.Exp)
            third_round = attention(G2, False)
            filled(eng, PAIRS, 4, third_round)

            def edge_weights(g, scores, weights, used):
                eng.wait_ge(L3["lk"], at(g))
                eng.wait_ge(L3["pv"], at(g, used))
                eng.activation(weights, scores, ACT.Sigmoid).then_inc(L3["al"], 1)

            def one_kind(p, h, live):
                if live(0):
                    for u in range(2):
                        g = p * 2 + u
                        eng.wait_ge(L3["e"], at(g))
                        eng.wait_ge(L3["al"], at(g, 2))
                        copy(WK[:, 6 + u, :], PS[:, u, :], 0.2).then_inc(L3["small"], 1)
                if live(2):
                    norm(L3, p - 2, h)
                if live(0):
                    for u in range(2):
                        edge_weights(p * 2 + u, WK[:, 6 + u, :], WK[:, 10 + u, :], 2)

            def all_kinds(p, h, live):
                if live(0):
                    for u in range(2):
                        edge_weights(p * 2 + u, WK[:, 10, :], WK[:, 10, :], 1)
                if live(1):
                    norm(L3, p - 1, 1 - h)

            def last_0():
                eng.preload_act_table(ACT.Sigmoid)
                early(one_kind, 2, 0)()

            eng.wait_ge(s_other, 1)
            more = eng.value_load(other[0:1, 0:1], min_val=0, max_val=1)
            with eng.If(more == 0):
                eng.preload_act_table(ACT.Exp)
                drained(PAIRS, 4, third_round, (lambda: None, last_0, early(one_kind, 2, 1)))
                for u in range(2):
                    eng.wait_ge(G2["xc"][0][u], DONE)
                pipelined2(eng, PAIRS, 2, one_kind, 2)
            with eng.Else():
                eng.preload_act_table(ACT.Exp)
                drained(PAIRS, 4, third_round)
                for u in range(2):
                    eng.wait_ge(G2["xc"][0][u], DONE)
                eng.preload_act_table(ACT.Sigmoid)
                pipelined2(eng, PAIRS, 1, all_kinds)

        @block.vector
        def _(eng):
            def stt(o, a, s, b, op0, op1):
                return eng.scalar_tensor_tensor(out=o, in0=a, scalar=s, in1=b, op0=op0, op1=op1)

            tt = eng.tensor_tensor

            def ln_sums(S, p, h):
                for u in range(2):
                    eng.wait_ge(S["y"], at(p * 2 + u))
                    for b in range(GB):
                        last = eng.bn_stats(stats[:, h, u * GB + b, :], ln_slots(S, h)[1][u][:, cols(b)])
                last.then_inc(S["bn"], 1)

            def ln_parts(S, p, h):
                even_mean, even_sq, odd_mean, odd_sq = (stats[:, h, :, k] for k in (1, 2, 4, 5))
                eng.wait_ge(S["bn"], at(p))
                tt(mdif[:, h, :], even_mean, odd_mean, ALU.subtract)
                tt(msum[:, h, :], even_mean, odd_mean, ALU.add)
                tt(sq[:, h, :], even_sq, odd_sq, ALU.add).then_inc(S["part"], 1)

            def ln_square(S, p, h):
                eng.wait_ge(S["part"], at(p))
                stt(mdif2[:, h, :], mdif[:, h, :], P / 4.0, mdif[:, h, :], ALU.mult, ALU.mult)
                eng.tensor_scalar(mean[:, h, :], msum[:, h, :], 0.5, None, ALU.mult).then_inc(S["mean"], 1)

            def ln_total(S, p, h):
                eng.wait_ge(S["mean"], at(p))
                stt(pvar[:, h, :], sq[:, h, :], P * EPS, mdif2[:, h, :], ALU.add, ALU.add).then_inc(S["agg"], 1)

            def ln_stats(S, p, h):
                for part in (ln_sums, ln_parts, ln_square, ln_total):
                    part(S, p, h)

            def ln_norm(S, i):
                eng.wait_ge(S["rstd"], at(i))
                for u in range(2):
                    eng.wait_ge(S["xc"][0][u], i * 16 + 16)
                    for b in range(GB):
                        k = u * GB + b
                        last = eng.tensor_scalar(XS[0][u][:, cols(b)], Y[0][u][:, cols(b)], mean[:, 0, k:k + 1],
                                                 rstd[:, 0, k:k + 1], ALU.subtract, ALU.mult)
                    last.then_inc(S["norm"], 1)

            credit(eng, I, "a1 z2 kev xtl")
            credit(eng, G0, "leaky gmx nmx rden y bn part mean agg norm")
            credit(eng, GR, "t1 t2 h ql hl nev")
            credit(eng, L1, "y bn part mean agg xtl z2f")
            credit(eng, G2, "leaky gmx nmx rden whev neg y bn part mean agg norm")
            credit(eng, L3, "g c lk y bn part mean agg")
            eng.sem_inc(GR["hl"], NG)
            eng.sem_inc(GR["nev"], NG)

            eng.memset(zer, 0.0).then_inc(s_b, 1)
            eng.wait_ge(s_w, 16 * NSMALL)
            eng.wait_ge(s_b, 1)
            for v in range(4):
                last = eng.tensor_scalar(abc[:, cols(v)], zer, acol[:, v:v + 1], None, ALU.add)
            last.then_inc(s_abc, 1)
            tt(brz[:], bcol[:, 0:2], bcol[:, 3:5], ALU.add).then_inc(s_b, 1)
            eng.tensor_scalar(bhn[:], bcol[:, 5:6], WS, None, ALU.mult).then_inc(s_b, 1)
            eng.wait_ge(s_hi, 3)
            stt(WR[:, 0, 1, :], rawT[:, 0:P], WS, WR[:, 0, 0, :], ALU.mult, ALU.subtract).then_inc(s_lo, 1)
            stt(WR[:, 1, 1, :], raw[:, P:2 * P], WS, WR[:, 1, 0, :], ALU.mult, ALU.subtract).then_inc(s_lo, 1)
            stt(HW[:, 1, :], rawT[:, RH * P:RL * P], WS, HW[:, 0, :], ALU.mult, ALU.subtract).then_inc(s_lo, 1)
            eng.wait_ge(s_hi, 6)
            stt(CW[:, :, 1, :], PS[:, 3:6, 0:GATES], WS, CW[:, :, 0, :], ALU.mult, ALU.subtract).then_inc(s_lo, 1)
            prod = PS[:, 6, :].rearrange("p (g v n) -> p g v n", g=2, v=2)
            stt(U1[:, :, 1, :], prod[:, :, 0, :], WS, U1[:, :, 0, :], ALU.mult, ALU.subtract).then_inc(s_lo, 1)
            stt(U2[:, :, 1, :], prod[:, :, 1, :], WS, U2[:, :, 0, :], ALU.mult, ALU.subtract).then_inc(s_lo, 1)

            def in_round(p, h, live):
                if live(0):
                    for u in range(2):
                        g = p * 2 + u
                        a = ADJ[h][u].bitcast(I32)
                        eng.wait_ge(s_adj[h][u], stored(p, h))
                        eng.tensor_scalar(A1[:, g, :], a, 0.0, None, ALU.not_equal).then_inc(I["a1"], 1)
                        eng.tensor_scalar(Z2[:, g, :], a, 0.0, None, ALU.is_le).then_inc(I["z2"], 1)
                if live(1):
                    for u in range(2):
                        g = (p - 1) * 2 + u
                        eng.wait_ge(I["kt"], at(g))
                        eng.tensor_scalar(CT[:, g, :], PS[:, u, 0:GW // 2].bitcast(F16), KINDS + 1.0, 0.0, ALU.min, ALU.max).then_inc(I["kev"], 1)
                    for u in range(2):
                        g = (p - 1) * 2 + u
                        eng.wait_ge(I["xth"], at(g))
                        tt(TP[:, g, 1, :], PS[:, 2 + u, :], TP[:, g, 0, :], ALU.subtract).then_inc(I["xtl"], 1)
            pipelined2(eng, PAIRS, 1, in_round)


            def attention(S, first):
                def round_(i, live):
                    if live(0):
                        for u in range(2):
                            g = i * 2 + u
                            eng.wait_ge(S["small"], at(g))
                            eng.wait_ge(S["exp"], at(g, 2))
                            tt(WK[:, 4 + u, :], PS[:, u, :], WK[:, 4 + u, :], ALU.max).then_inc(S["leaky"], 1)
                        for u in range(2):
                            g = i * 2 + u
                            eng.wait_ge(S["leaky"], at(g))
                            eng.tensor_reduce(gmx[:, u * GB:(u + 1) * GB], b4(WK[:, 4 + u, :]), AX.X, ALU.max).then_inc(S["gmx"], 1)
                    if live(1):
                        eng.wait_ge(S["exp"], at(i * 2 - 1))
                        eng.reciprocal(rden[:], den[:]).then_inc(S["rden"], 1)
                    if live(0):
                        eng.wait_ge(S["gmx"], at(i * 2 + 1))
                        eng.tensor_scalar(nmx[:], gmx[:], -1.0 / WS, None, ALU.mult).then_inc(S["nmx"], 1)
                    if first:
                        if live(2):
                            eng.wait_ge(S["xl"], at((i - 2) * 2 + 1, 2))
                            ln_norm(S, i - 2)
                        if live(1):
                            eng.wait_ge(S["rden"], at(i - 1))
                            for u in range(2):
                                g = (i - 1) * 2 + u
                                eng.wait_ge(S["pv"], at(g))
                                eng.wait_ge(S["norm"], at(g, 2))
                                for b in range(GB):
                                    k = u * GB + b
                                    last = stt(Y[0][u][:, cols(b)], PS[:, 6 + u, cols(b)], rden[:, k:k + 1], X[:, g, b, :], ALU.mult, ALU.add)
                                last.then_inc(S["y"], 1)
                            ln_stats(S, i - 1, 0)
                    else:
                        if live(0):
                            for u in range(2):
                                g = i * 2 + u
                                eng.wait_ge(S["wh"], at(g))
                                eng.wait_ge(S["pv"], at(g, 2))
                                eng.tensor_scalar(WK[:, 10 + u, :], PS[:, 2 + u, :], 1.0 / WS, None, ALU.mult).then_inc(S["whev"], 1)
                        if live(3):
                            eng.wait_ge(S["tr"], at((i - 3) * 2 + 1, 2))
                            ln_norm(S, i - 3)
                        if live(2):
                            for u in range(2):
                                g = (i - 2) * 2 + u
                                eng.wait_ge(S["eu"], at(g))
                                eng.wait_ge(S["res"], at(g))
                                eng.wait_ge(S["norm"], at(g, 2))
                                stt(Y[0][u], WK[:, 14 + u, :], -1.0, WK[:, 12 + u, :], ALU.add, ALU.add).then_inc(S["y"], 1)
                            ln_stats(S, i - 2, 0)
                        if live(1):
                            for u in range(2):
                                g = (i - 1) * 2 + u
                                eng.wait_ge(S["ru"], at(g))
                                eng.tensor_scalar(WK[:, 14 + u, :], WK[:, 12 + u, :], 0.0, None, ALU.min).then_inc(S["neg"], 1)
                return round_

            def gru_round(j, live, back, norm_part=None, kinds=False):
                for u in range(2):
                    if live(0):
                        t = j * 2 + u
                        eng.wait_ge(GR["qh"], at(t))
                        qh, ql = message(j, u)
                        tt(ql, PS[:, u, :], qh, ALU.subtract).then_inc(GR["ql"], 1)
                    if live(1):
                        t = (j - 1) * 2 + u
                        eng.wait_ge(GR["r"], at(t))
                        eng.wait_ge(GR["hn"], at(t))
                        stt(WK[:, 8 + u, :], PS[:, 6, :], bhn[:, 0:1], WK[:, 8 + u, :], ALU.add, ALU.mult).then_inc(GR["t1"], 1)
                        eng.wait_ge(GR["t1"], at(t))
                        eng.wait_ge(GR["gi"], at(t))
                        tt(WK[:, 8 + u, :], PS[:, 7, :], WK[:, 8 + u, :], ALU.add).then_inc(GR["t2"], 1)
                    if live(2 - u):
                        t = (j - 1) * 2 + u - 1
                        g = ((j - 2 + u) % PAIRS) * 2 + (1 - u)
                        eng.wait_ge(GR["zd"], at(t))
                        tt(HT[:, g, :], WK[:, 6 + (1 - u), :], WK[:, 10 + (1 - u), :], ALU.add).then_inc(GR["h"], 1)
                    if norm_part:
                        norm_part(u, 0)
                    if back:
                        t = (j - 2) * 2 + u
                        g = ((j - 2) % PAIRS) * 2 + u
                        eng.wait_ge(GR["tr"], at(t))
                        eng.tensor_copy(NP[:, g].rearrange("p s n -> p (s n)"), PS[:, 2 + u, :].bitcast(F16)).then_inc(GR["nev"], 1)
                    if live(2 - u):
                        t = (j - 1) * 2 + u - 1
                        g = ((j - 2 + u) % PAIRS) * 2 + (1 - u)
                        eng.wait_ge(GR["hh"], at(t))
                        tt(TP[:, g, 1, :], HT[:, g, :], TP[:, g, 0, :], ALU.subtract).then_inc(GR["hl"], 1)
                    if norm_part:
                        norm_part(u, 1)

            def norm_step(p, h, u, live, part=None):
                if live(0) and part != 1:
                    g = p * 2 + u
                    if not live(1) and u == 0:
                        for v in range(2):
                            eng.wait_ge(G0["xc"][0][v], DONE)
                    eng.wait_ge(L1["sum"], at(g))
                    tt(HT[:, g, :], PS[:, 2, :], flat(X[:, g]), ALU.add).then_inc(L1["y"], 1)
                    eng.wait_ge(L1["y"], at(g))
                    eng.tensor_copy(NP[:, g, 0, :], Z2[:, g, :]).then_inc(L1["z2f"], 1)
                    for b in range(GB):
                        last = eng.bn_stats(stats[:, h, u * GB + b, :], HT[:, g, cols(b)])
                    if u:
                        last.then_inc(L1["bn"], 1)
                        for step in (ln_parts, ln_square, ln_total):
                            step(L1, p, h)
                if live(2) and part != 0:
                    g = (p - 2) * 2 + u
                    eng.wait_ge(L1["xth"], at(g))
                    tt(TP[:, g, 1, :], PS[:, 3, :], TP[:, g, 0, :], ALU.subtract).then_inc(L1["xtl"], 1)

            eng.wait_ge(I["tr"], ALL)
            pipelined(eng, PAIRS, 3, attention(G0, True), gru_first(gru_round))
            gru_pipelined(eng, gru_round, norm_step)

            eng.wait_ge(s_ksum, 1)
            eng.tensor_reduce(kall[:], PS[:, 7, 0:NG], AX.X, ALU.add).then_inc(s_kred, 1)
            eng.wait_ge(s_kred, 1)
            eng.tensor_scalar(other[:], kall[:], 0.25 * B * P * P, None, ALU.is_gt).then_inc(s_other, 1)

            for h in range(2):
                for u in range(2):
                    eng.wait_ge(L1["xc"][h][u], HALF_DONE)
            third_round = attention(G2, False)
            filled(eng, PAIRS, 3, third_round)


            def sums(p, h):
                for u in range(2):
                    g = p * 2 + u
                    eng.wait_ge(L3["xb"], at(g))
                    eng.wait_ge(L3["pv"], at(g))
                    eng.wait_ge(L3["norm"], at(g, 4))
                    tt(ln_slots(L3, h)[1][u], PS[:, 4 + u, :], WK[:, 8 + u, :], ALU.add).then_inc(L3["y"], 1)
                ln_stats(L3, p, h)

            def one_kind(p, h, live):
                if live(1):
                    for u in range(2):
                        g = (p - 1) * 2 + u
                        eng.wait_ge(L3["small"], at(g))
                        tt(WK[:, 6 + u, :], PS[:, u, :], WK[:, 6 + u, :], ALU.max).then_inc(L3["lk"], 1)
                if live(0):
                    for u in range(2):
                        g = p * 2 + u
                        eng.wait_ge(G2["ht"], at(g))
                        eng.wait_ge(L3["e"], at(g, 2))
                        eng.tensor_scalar(WK[:, 4 + u, :], HT[:, g, :], kcol[:, 0:1], None, ALU.mult).then_inc(L3["g"], 1)
                if live(2):
                    sums(p - 2, h)

            def all_kinds(p, h, live):
                if live(0):
                    for u in range(2):
                        g = p * 2 + u
                        eng.wait_ge(L3["e"], at(g, 1))
                        for k in range(KINDS):
                            last = eng.tensor_scalar(WK[:, 4 + k, :], HT[:, g, :], kcol[:, k:k + 1], None, ALU.mult)
                        last.then_inc(L3["g"], 1)
                        sc, tmp, kinds = WK[:, 10, :], WK[:, 11, :], CT[:, g, :]
                        eng.wait_ge(L3["e"], at(g))
                        eng.wait_ge(L3["pv"], at(g, 1))
                        steps = 2 * KINDS + 3
                        done = g * steps + CREDIT
                        stt(sc, kinds, 1.0, PS[:, 0, :], ALU.is_equal, ALU.mult).then_inc(L3["c"], 1)
                        for k in range(1, KINDS):
                            stt(tmp, kinds, k + 1.0, PS[:, k, :], ALU.is_equal, ALU.mult).then_inc(L3["c"], 1)
                            eng.wait_ge(L3["c"], done + (2 * k))
                            tt(sc, sc, tmp, ALU.add).then_inc(L3["c"], 1)
                            eng.wait_ge(L3["c"], done + (2 * k + 1))
                        for n, k in enumerate((0.0, KINDS + 1.0)):
                            eng.tensor_scalar(tmp, kinds, k, MASKED, ALU.is_equal, ALU.mult).then_inc(L3["c"], 1)
                            eng.wait_ge(L3["c"], done + (2 * KINDS + 2 * n))
                            tt(sc, sc, tmp, ALU.add).then_inc(L3["c"], 1)
                            eng.wait_ge(L3["c"], done + (2 * KINDS + 2 * n + 1))
                        stt(sc, sc, 0.2, sc, ALU.mult, ALU.max).then_inc(L3["lk"], 1)
                    sums(p, h)

            more = eng.value_load(other[0:1, 0:1], min_val=0, max_val=1)
            with eng.If(more == 0):
                drained(PAIRS, 3, third_round, [early(one_kind, 2, p) for p in range(2)])
                pipelined2(eng, PAIRS, 2, one_kind, 2)
            with eng.Else():
                drained(PAIRS, 3, third_round)
                eng.wait_ge(G2["ht"], ALL)
                pipelined2(eng, PAIRS, 0, all_kinds)

        @block.gpsimd
        def _(eng):
            tt = eng.tensor_tensor
            eng.memset(idf[:], 0.0).then_inc(s_id, 1)
            eng.memset(idh[:], 0.0).then_inc(s_id, 1)
            eng.memset(maskI[:], 0.0).then_inc(s_id, 1)
            eng.memset(rootp[:], float(P) ** 0.5)
            eng.memset(nroot[:], -float(P) ** 0.5)
            eng.memset(mhalf[:], -0.5)
            eng.memset(mone[:], -1.0)
            eng.memset(ones[:], 1.0).then_inc(s_id, 1)
            eng.memset(half[:], -0.5).then_inc(s_id, 1)
            eng.wait_ge(s_id, 5)
            for m, v in ((idf, 1.0), (idh, 1.0), (maskI, MASKED)):
                eng.affine_select(out=m[:], in_=m[:], compare_op=ALU.not_equal, fill=v, base=0,
                                  pattern=[[-1, P]], channel_multiplier=1).then_inc(s_id, 1)
            credit(eng, I, "xs")
            credit(eng, G0, "pw rstd xl ht")
            credit(eng, GR, "d zd")
            credit(eng, L1, "pw rstd shift")
            credit(eng, G2, "pw rstd relu res")
            credit(eng, L3, "xb pw rstd shift")

            with eng.Fori(0, PAIRS // 2) as i:
                for h in range(2):
                    for u in range(2):
                        g = i * 4 + (2 * h + u)
                        eng.wait_ge(s_x[h][u], i * 16 + 16)
                        eng.wait_ge(I["tr"], at(g, 2))
                        eng.tensor_copy(XS[0][u], flat(X[:, g])).then_inc(I["xs"], 1)

            def ln_rstd(S, p, h, shifted=False):
                eng.wait_ge(S["agg"], at(p))
                tt(ipow[:, h, :], pvar[:, h, :], half[:], ALU.pow).then_inc(S["pw"], 1)
                eng.wait_ge(S["pw"], at(p))
                if shifted:
                    tt(nrstd[:, h, :], ipow[:, h, :], nroot[:], ALU.mult)
                tt(rstd[:, h, :], ipow[:, h, :], rootp[:], ALU.mult).then_inc(S["rstd"], 1)
                if shifted:
                    eng.wait_ge(S["rstd"], at(p))
                    tt(shift[:, h, :], mean[:, h, :], nrstd[:, h, :], ALU.mult).then_inc(S["shift"], 1)

            def first_round(i, live):
                if live(3):
                    for u in range(2):
                        g = (i - 3) * 2 + u
                        eng.wait_ge(G0["tev"], at(g))
                        tt(HT[:, g, :], TP[:, g, 0, :], TP[:, g, 1, :], ALU.add).then_inc(G0["ht"], 1)
                if live(2):
                    for u in range(2):
                        g = (i - 2) * 2 + u
                        eng.wait_ge(G0["xh"], at(g))
                        tt(NP[:, g, 1, :], XS[0][u], NP[:, g, 0, :], ALU.subtract).then_inc(G0["xl"], 1)
                if live(1):
                    ln_rstd(G0, i - 1, 0)

            def gru_round(j):
                for u in range(2):
                    t = j * 2 + u
                    g = (j % PAIRS) * 2 + u
                    eng.wait_ge(GR["n"], at(t))
                    eng.wait_ge(GR["h"], at(t, 2))
                    tt(WK[:, 10 + u, :], HT[:, g, :], WK[:, 6 + u, :], ALU.subtract).then_inc(GR["d"], 1)
                    eng.wait_ge(GR["d"], at(t))
                    eng.wait_ge(GR["z"], at(t))
                    tt(WK[:, 10 + u, :], WK[:, 10 + u, :], WK[:, 4 + u, :], ALU.mult).then_inc(GR["zd"], 1)

            pipelined(eng, PAIRS, 3, first_round, (lambda: None, lambda: gru_round(0)))
            with eng.Fori(1, LAST_ROUND - 1) as j:
                gru_round(j)
            with eng.Fori(LAST_ROUND // 2, LAYERS * PAIRS // 2) as i:
                for h in range(2):
                    gru_round(i * 2 + (h - 1))
                    ln_rstd(L1, i * 2 + (h - LAST_ROUND), h, shifted=True)
            for h in range(2):
                if h == 0:
                    gru_round(LAYERS * PAIRS - 1)
                ln_rstd(L1, PAIRS - 2 + h, h, shifted=True)

            def third_round(i, live):
                if live(2):
                    ln_rstd(G2, i - 2, 0)
                if live(1):
                    for u in range(2):
                        g = (i - 1) * 2 + u
                        eng.wait_ge(G2["neg"], at(g))
                        tt(WK[:, 12 + u, :], WK[:, 12 + u, :], WK[:, 14 + u, :], ALU.subtract).then_inc(G2["relu"], 1)
                    for u in range(2):
                        g = (i - 1) * 2 + u
                        eng.wait_ge(G2["relu"], at(g))
                        tt(WK[:, 12 + u, :], WK[:, 12 + u, :], flat(X[:, g]), ALU.add).then_inc(G2["res"], 1)
            def last_round(p, h, live):
                if live(0):
                    for u in range(2):
                        g = p * 2 + u
                        eng.wait_ge(L3["y"], at(g, 2))
                        tt(b4(WK[:, 8 + u, :]), X[:, g], bias_all[:, None, :].to_broadcast([P, GB, P]), ALU.add).then_inc(L3["xb"], 1)
                if live(1):
                    ln_rstd(L3, p - 1, 1 - h, shifted=True)

            def last_0():
                eng.wait_ge(G2["pv"], ALL)
                for u in range(2):
                    eng.wait_ge(G2["xc"][0][u], 16 + 16)
                early(last_round, 1, 0)()

            pipelined(eng, PAIRS, 2, third_round, [last_0])
            for u in range(2):
                eng.wait_ge(G2["xc"][0][u], DONE)
            pipelined2(eng, PAIRS, 1, last_round, 1)


_INS = ['x', 'adj', 'L0_gnn_W', 'L0_gnn_a', 'L1_gnn_weight', 'L1_gnn_w_ih', 'L1_gnn_w_hh', 'L1_gnn_b_ih', 'L1_gnn_b_hh',
        'L2_gnn_W', 'L2_gnn_a', 'L3_gnn_a0', 'L3_gnn_a1', 'L3_gnn_a2', 'L3_gnn_a3', 'L3_gnn_bias']
_OUTS = [((B, P, P), 'float32')]


def kernel(**inputs):
    import numpy as _np
    import concourse.bacc as _bacc
    from concourse import mybir as _mybir
    from concourse.bass_utils import run_bass_kernel_spmd as _run

    nc = _bacc.Bacc("TRN2", target_bir_lowering=False, num_devices=1)
    arrays, args = {}, []
    for name in _INS:
        a = _np.ascontiguousarray(inputs[name])
        arrays[f"in_{name}_dram"] = a
        args.append(nc.dram_tensor(f"in_{name}_dram", a.shape, _mybir.dt.from_np(a.dtype), kind="ExternalInput").ap())
    for i, (shape, dtype) in enumerate(_OUTS):
        dt = _mybir.dt.from_np(_np.dtype(dtype))
        args.append(nc.dram_tensor(f"out_{i}_dram", shape, dt, kind="ExternalOutput").ap())
    graph_kernel(nc, *args)
    r = _run(nc, [arrays], core_ids=[0])
    return r.results[0]["out_0_dram"]
```
